# Optimizing a Trainium2 kernel written in Bass

```python
import numpy as np
import jax
import jax.numpy as jnp

def _softmax(x, axis=-1):
    return jax.nn.softmax(x, axis=axis)
def _gelu(x):
    return jax.nn.gelu(x, approximate=True)
def _silu(x):
    return jax.nn.silu(x)
def _sigmoid(x):
    return jax.nn.sigmoid(x)
def _layernorm(x, axis=-1, eps=1e-5):
    m = jnp.mean(x, axis=axis, keepdims=True)
    v = jnp.var(x, axis=axis, keepdims=True)
    return (x - m) / jnp.sqrt(v + eps)
def _scatter_add(tgt, idx, src, axis=0):
    return tgt.at[idx].add(src)
def _segment_sum(src, seg, n):
    return jax.ops.segment_sum(src, seg, n)

kernel_name = 'mk_conv_preact_d2_conv_nhwc128_fc1e4b'

def setup_inputs(seed: int = 0):
    np.random.seed(seed)
    _w = jnp.asarray
    def _rec_inputs():
        import jax
        import jax.numpy as jnp
        _gk = jax.random.key(seed)
        x = 7.22e-05 + 1 * jax.random.normal(jax.random.fold_in(_gk, 1), (4, 128, 128, 128), jnp.float32)
        return x
    x = _rec_inputs()
    def _L0_conv_setup():
        import jax, jax.numpy as jnp
        import numpy as np
        K = 3
        PAD = 1
        HEADS = 4
        C = 128
        K2 = K * K

        def _csa(x, w_qkv, w_v, w_proj):
            B, H, W, Cc = x.shape
            hd = Cc // HEADS
            scale = hd ** (-0.5)
            N = H * W
            att = jnp.einsum('bhwc,oc->bhwo', x, w_qkv)
            att = att.reshape(B, N, HEADS, K2, K2).transpose(0, 2, 1, 3, 4)
            att = jax.nn.softmax(att * scale, axis=-1)
            xp = jnp.pad(x, ((0, 0), (PAD, PAD), (PAD, PAD), (0, 0)))
            patches = jnp.stack([xp[:, di:di + H, dj:dj + W, :] for di in range(K) for dj in range(K)], axis=3)
            v = patches.reshape(B, N, K2, Cc)
            v = jnp.einsum('pij,bnpj->bnpi', w_v, v)
            v = v.reshape(B, N, K2, HEADS, hd).transpose(0, 3, 1, 2, 4)
            out = jnp.einsum('bhnpq,bhnqd->bhnpd', att, v)
            out = out.transpose(0, 1, 4, 3, 2).reshape(B, Cc, K2, H, W)
            acc = jnp.zeros((B, Cc, H + 2 * PAD, W + 2 * PAD), x.dtype)
            p = 0
            for di in range(K):
                for dj in range(K):
                    acc = acc.at[:, :, di:di + H, dj:dj + W].add(out[:, :, p])
                    p += 1
            y = acc[:, :, PAD:PAD + H, PAD:PAD + W].transpose(0, 2, 3, 1)
            return jnp.einsum('bhwc,oc->bhwo', y, w_proj)
        key = jax.random.key(seed)
        k1, k2, k3, k4 = jax.random.split(key, 4)
        B, H, W = (4, 128, 128)
        x = jax.random.normal(k1, (B, H, W, C), jnp.float32)
        w_qkv = jax.random.normal(k2, (K2 * K2 * HEADS, C), jnp.float32) * 0.02
        w_v = jax.random.normal(k3, (K2, C, C), jnp.float32) * np.sqrt(2.0 / (K2 * C))
        w_proj = jax.random.normal(k4, (C, C), jnp.float32) * 0.02
        return {'x': x, 'w_qkv': w_qkv, 'w_v': w_v, 'w_proj': w_proj}
    _L0_conv_all = _L0_conv_setup()
    _L0_conv_in = {k: v for k, v in _L0_conv_all.items() if k in ('w_qkv', 'w_v', 'w_proj', )}
    del _L0_conv_all

    def _L1_conv_setup():
        import jax, jax.numpy as jnp
        import numpy as np
        from jax import lax
        EPS = 0.001

        def _sign_pm1(v):
            return jnp.where(v >= 0, jnp.ones_like(v), -jnp.ones_like(v))
        key = jax.random.key(seed)
        k1, k2 = jax.random.split(key)
        B, H, Wd, Cin, Cout, KS = (32, 56, 56, 128, 128, 3)
        x = jax.random.normal(k1, (B, H, Wd, Cin), dtype=jnp.float32)
        gamma = jnp.ones((Cin,), dtype=jnp.float32)
        beta = jnp.zeros((Cin,), dtype=jnp.float32)
        W = jax.random.normal(k2, (KS, KS, Cin, Cout), dtype=jnp.float32) * 0.1
        return {'x': x, 'gamma': gamma, 'beta': beta, 'W': W}
    _L1_conv_all = _L1_conv_setup()
    _L1_conv_in = {k: v for k, v in _L1_conv_all.items() if k in ('gamma', 'beta', 'W', )}
    del _L1_conv_all

    return {
        "x": x,
        "L0_conv_w_qkv": _L0_conv_in["w_qkv"],
        "L0_conv_w_v": _L0_conv_in["w_v"],
        "L0_conv_w_proj": _L0_conv_in["w_proj"],
        "L1_conv_gamma": _L1_conv_in["gamma"],
        "L1_conv_beta": _L1_conv_in["beta"],
        "L1_conv_W": _L1_conv_in["W"],
    }

def reference(x, L0_conv_w_qkv, L0_conv_w_v, L0_conv_w_proj, L1_conv_gamma, L1_conv_beta, L1_conv_W):
    import jax
    import jax.numpy as jnp
    def _L0_conv_ref(x, w_qkv, w_v, w_proj):
        import jax, jax.numpy as jnp
        import numpy as np
        K = 3
        PAD = 1
        HEADS = 4
        C = 128
        K2 = K * K

        def _csa(x, w_qkv, w_v, w_proj):
            B, H, W, Cc = x.shape
            hd = Cc // HEADS
            scale = hd ** (-0.5)
            N = H * W
            att = jnp.einsum('bhwc,oc->bhwo', x, w_qkv)
            att = att.reshape(B, N, HEADS, K2, K2).transpose(0, 2, 1, 3, 4)
            att = jax.nn.softmax(att * scale, axis=-1)
            xp = jnp.pad(x, ((0, 0), (PAD, PAD), (PAD, PAD), (0, 0)))
            patches = jnp.stack([xp[:, di:di + H, dj:dj + W, :] for di in range(K) for dj in range(K)], axis=3)
            v = patches.reshape(B, N, K2, Cc)
            v = jnp.einsum('pij,bnpj->bnpi', w_v, v)
            v = v.reshape(B, N, K2, HEADS, hd).transpose(0, 3, 1, 2, 4)
            out = jnp.einsum('bhnpq,bhnqd->bhnpd', att, v)
            out = out.transpose(0, 1, 4, 3, 2).reshape(B, Cc, K2, H, W)
            acc = jnp.zeros((B, Cc, H + 2 * PAD, W + 2 * PAD), x.dtype)
            p = 0
            for di in range(K):
                for dj in range(K):
                    acc = acc.at[:, :, di:di + H, dj:dj + W].add(out[:, :, p])
                    p += 1
            y = acc[:, :, PAD:PAD + H, PAD:PAD + W].transpose(0, 2, 3, 1)
            return jnp.einsum('bhwc,oc->bhwo', y, w_proj)
        return _csa(x, w_qkv, w_v, w_proj)

    def _L1_conv_ref(x, gamma, beta, W):
        import jax, jax.numpy as jnp
        import numpy as np
        from jax import lax
        EPS = 0.001

        def _sign_pm1(v):
            return jnp.where(v >= 0, jnp.ones_like(v), -jnp.ones_like(v))
        axes = (0, 1, 2)
        mean = jnp.mean(x, axis=axes, keepdims=True)
        var = jnp.var(x, axis=axes, keepdims=True)
        x_hat = (x - mean) * lax.rsqrt(var + EPS)
        out_bn = gamma * x_hat + beta
        x_bin = _sign_pm1(out_bn)
        scale = jnp.mean(jnp.abs(W), axis=(0, 1, 2))
        W_bin = _sign_pm1(W) * scale
        x_pad = jnp.pad(x_bin, ((0, 0), (1, 1), (1, 1), (0, 0)), constant_values=1.0)
        out = lax.conv_general_dilated(x_pad, W_bin, window_strides=(1, 1), padding='VALID', dimension_numbers=('NHWC', 'HWIO', 'NHWC'))
        return out

    def _gn(v, G=32, eps=1e-5):
        B_, H_, W_, C_ = v.shape
        g = v.reshape(B_, H_, W_, G, C_ // G)
        m = jnp.mean(g, axis=(1, 2, 4), keepdims=True)
        s = jnp.var(g, axis=(1, 2, 4), keepdims=True)
        return ((g - m) / jnp.sqrt(s + eps)).reshape(v.shape)

    def _ln_c(v, eps=1e-6):
        m = jnp.mean(v, axis=-1, keepdims=True)
        s = jnp.var(v, axis=-1, keepdims=True)
        return (v - m) / jnp.sqrt(s + eps)

    def _ln_t(v, eps=1e-5):
        m = jnp.mean(v, axis=-1, keepdims=True)
        s = jnp.var(v, axis=-1, keepdims=True)
        return (v - m) / jnp.sqrt(s + eps)

    def _to_tokens(v):
        B_, H_, W_, C_ = v.shape
        return v.reshape(B_, H_ * W_, C_)
    def _from_tokens(t, like):
        return t.reshape(like.shape)

    x = x + _L0_conv_ref(_gn(x), L0_conv_w_qkv, L0_conv_w_v, L0_conv_w_proj)
    x = x + _L1_conv_ref(_gn(x), L1_conv_gamma, L1_conv_beta, L1_conv_W)
    return x


_drawn_inputs = setup_inputs


def setup_inputs(seed=0):
    import zlib

    import numpy as np

    out = dict(_drawn_inputs(seed))
    spreads = {'L1_conv_gamma': (1.0, 0.2), 'L1_conv_beta': (0.0, 0.1)}
    factors = {}
    for name, (base, spread) in spreads.items():
        noise = np.random.default_rng([zlib.crc32(name.encode()), seed]).standard_normal(out[name].shape)
        drawn = base * np.exp(spread * noise) if base else spread * noise
        out[name] = jnp.asarray(drawn.astype(out[name].dtype))
    for name, factor in factors.items():
        out[name] = (out[name] * factor).astype(out[name].dtype)
    return out
```

```python
from contextlib import ExitStack

import concourse.bass as bass
from concourse import mybir

ALU = mybir.AluOpType
ACT = mybir.ActivationFunctionType
AX = mybir.AxisListType
F32 = mybir.dt.float32
F16 = mybir.dt.float16
U32 = mybir.dt.uint32

P = 128
W = 128
C = 128
HEADS = 4
HD = C // HEADS
K2 = 9
NPH = 3 * 3 * HEADS
LOG = K2 * NPH
JT = 13
KT = JT * K2
TILES = 10
WP = JT * TILES
WIN = JT + 2
WC = NPH // 3 * 2
RING = 8
EPS_GN = 1e-5
EPS_BN = 1e-3


def norm_params(nc, tag, B, n_group, n_chan, eps, sums, sqs, ones, group, scale, bias, bn=None):
    with ExitStack() as c:
        def sb(name, shape):
            return c.enter_context(nc.sbuf_tensor(f"{tag}_{name}", shape, F32))

        cols, stat, tmp, root, q2, r2 = (sb(n, [P, 2 * B]) for n in ("cols", "stat", "tmp", "root", "q2", "r2"))
        one = sb("one", [P, 8])
        ps_c = c.enter_context(nc.psum_tensor(f"{tag}_ps_c", [P, 512], F32))
        ps_g = c.enter_context(nc.psum_tensor(f"{tag}_ps_g", [P, 512], F32))
        s_cols = c.enter_context(nc.semaphore(f"{tag}_cols_summed"))
        s_colc = c.enter_context(nc.semaphore(f"{tag}_cols_copied"))
        s_grp = c.enter_context(nc.semaphore(f"{tag}_groups_summed"))
        s_var = c.enter_context(nc.semaphore(f"{tag}_variance"))
        s_root = c.enter_context(nc.semaphore(f"{tag}_root"))
        s_chain = c.enter_context(nc.semaphore(f"{tag}_chain"))
        with nc.Block() as block:
            @block.tensor
            def _(pe):
                for k, parts in enumerate((sums, sqs)):
                    for b in range(B):
                        for n, t in enumerate(parts):
                            last = pe.matmul(ps_c[:, k * B + b:k * B + b + 1], t[:, b, :], ones[0:t.shape[0], 0:1],
                                             start=n == 0, stop=n == len(parts) - 1)
                last.then_inc(s_cols, 1)
                pe.wait_ge(s_colc, 1)
                pe.matmul(ps_g[:, 0:2 * B], group[:], cols[:], start=True, stop=True).then_inc(s_grp, 1)

            @block.scalar
            def _(act):
                act.wait_ge(s_var, 1)
                act.activation(root[:, 0:B], tmp[:, 0:B], ACT.Sqrt).then_inc(s_root, 1)
                if bn is not None:
                    act.wait_ge(s_var, 2)
                    act.activation(root[:, 0:1], one[:, 3:4], ACT.Sqrt).then_inc(s_root, 1)

            @block.vector
            def _(dve):
                chain = [0]

                def link(ins):
                    chain[0] += 1
                    ins.then_inc(s_chain, 1)
                    dve.wait_ge(s_chain, chain[0])

                def rsqrt(dst, v, n):
                    link(dve.reciprocal(dst, root[:, 0:n]))
                    link(dve.tensor_tensor(r2[:, 0:n], dst, dst, ALU.mult))
                    link(dve.tensor_tensor(r2[:, 0:n], r2[:, 0:n], v, ALU.mult))
                    link(dve.tensor_scalar(r2[:, 0:n], r2[:, 0:n], -0.5, 1.5, ALU.mult, ALU.add))
                    link(dve.tensor_tensor(dst, dst, r2[:, 0:n], ALU.mult))

                dve.wait_ge(s_cols, 1)
                dve.tensor_copy(cols[:], ps_c[:, 0:2 * B]).then_inc(s_colc, 1)
                dve.wait_ge(s_grp, 1)
                link(dve.tensor_scalar(stat[:], ps_g[:, 0:2 * B], 1.0 / n_group, None, ALU.mult))
                m = stat[:, 0:B]
                link(dve.tensor_tensor(tmp[:, B:2 * B], m, m, ALU.mult))
                link(dve.tensor_tensor(tmp[:, 0:B], stat[:, B:2 * B], tmp[:, B:2 * B], ALU.subtract))
                link(dve.tensor_scalar(tmp[:, 0:B], tmp[:, 0:B], 0.0, eps, ALU.max, ALU.add))
                dve.tensor_copy(q2[:, 0:B], tmp[:, 0:B]).then_inc(s_var, 1)
                dve.wait_ge(s_root, 1)
                rsqrt(scale, q2[:, 0:B], B)
                link(dve.tensor_tensor(bias, m, scale, ALU.mult))
                link(dve.tensor_scalar(bias, bias, -1.0, None, ALU.mult))
                if bn is None:
                    return
                gamma, beta, bn_eps, a, t = bn
                link(dve.tensor_scalar(cols[:], cols[:], 1.0 / n_chan, None, ALU.mult))
                mu, q = cols[:, 0:B], cols[:, B:2 * B]
                link(dve.tensor_scalar(tmp[:, 0:B], mu, 2.0, None, ALU.mult))
                link(dve.tensor_tensor(tmp[:, 0:B], tmp[:, 0:B], m, ALU.subtract))
                link(dve.tensor_tensor(tmp[:, 0:B], tmp[:, 0:B], m, ALU.mult))
                link(dve.tensor_tensor(q2[:, B:2 * B], q, tmp[:, 0:B], ALU.subtract))
                link(dve.tensor_tensor(q2[:, B:2 * B], q2[:, B:2 * B], scale, ALU.mult))
                link(dve.tensor_tensor(q2[:, B:2 * B], q2[:, B:2 * B], scale, ALU.mult))
                link(dve.tensor_tensor(q2[:, 0:B], mu, m, ALU.subtract))
                link(dve.tensor_tensor(q2[:, 0:B], q2[:, 0:B], scale, ALU.mult))
                link(dve.tensor_reduce(one[:, 0:2], q2[:].rearrange("p (k b) -> p k b", k=2), AX.X, ALU.add))
                link(dve.tensor_scalar(one[:, 0:2], one[:, 0:2], 1.0 / B, None, ALU.mult))
                link(dve.tensor_tensor(one[:, 2:3], one[:, 0:1], one[:, 0:1], ALU.mult))
                link(dve.tensor_tensor(one[:, 3:4], one[:, 1:2], one[:, 2:3], ALU.subtract))
                dve.tensor_scalar(one[:, 3:4], one[:, 3:4], 0.0, bn_eps, ALU.max, ALU.add).then_inc(s_var, 1)
                dve.wait_ge(s_root, 2)
                rsqrt(one[:, 4:5], one[:, 3:4], 1)
                link(dve.tensor_tensor(one[:, 5:6], one[:, 4:5], gamma, ALU.mult))
                link(dve.tensor_tensor(one[:, 6:7], one[:, 5:6], one[:, 0:1], ALU.mult))
                link(dve.tensor_tensor(one[:, 7:8], one[:, 6:7], beta, ALU.subtract))
                link(dve.tensor_scalar(a, scale, one[:, 5:6], None, ALU.mult))
                link(dve.tensor_tensor(t, a, m, ALU.mult))
                link(dve.tensor_scalar(t, t, one[:, 7:8], None, ALU.add))


def build_kernel(nc, x, w_qkv, w_v, w_proj, gamma, beta, w_bin, out):
    B, H = x.shape[0], x.shape[1]
    ROWS = B * H
    NP = ROWS // 2
    IT = ROWS // 8
    IPI = H // 8
    NPIX = float(H * W * (C // 32))
    xr_v = x.rearrange("b h w c -> (b h) w c")
    out_v = out.rearrange("b h w c -> (b h) w c")
    CH = min(16, H // 4)
    NCH = H // CH
    xchunks = x.rearrange("b (k r) w c -> (b k) (r w c)", r=CH).rearrange("k (p n) -> k p n", p=P)
    x1_d = nc.dram_tensor("x1_scratch", [ROWS, W, C], F32).ap()
    v_d = nc.dram_tensor("v_scratch", [4, 2, WP, K2 * 256], F16).ap()
    a_d = nc.dram_tensor("a_scratch", [4, 2, WP, K2 * NPH * 2], F16).ap()

    def after(eng, sem, count):
        if isinstance(count, int) and count <= 0:
            return
        eng.wait_ge(sem, count)

    def place(i, u, d):
        return (u + d) % 4, i + (u + d) // 4

    def valid(i, u, d):
        return not isinstance(i, int) or 0 <= 4 * i + u + d < NP

    with ExitStack() as ctx:
        def sb(name, shape, dt, c=ctx):
            return c.enter_context(nc.sbuf_tensor(name, shape, dt))

        def sem(name, c=ctx):
            return c.enter_context(nc.semaphore(name))

        def psum(name, shape, dt, c):
            return c.enter_context(nc.psum_tensor(name, shape, dt))

        ident = sb("ident", [P, P], F32)
        ones = sb("ones", [P, P], F32)
        group = sb("group", [P, P], F32)
        gn_scale = sb("gn_scale", [P, B], F32)
        gn_bias = sb("gn_bias", [P, B], F32)
        acc_sum = sb("acc_sum", [P, B, 256], F32)
        acc_sq = sb("acc_sq", [P, B, 256], F32)
        wbin = sb("wbin", [P, K2, C], F16)
        neg_sum = sb("neg_sum", [1, C], F16)
        ones16 = sb("ones16", [1, P], F16)
        wscale = sb("wscale", [P, 4, C], F32)
        gam = sb("gam", [P, 1], F32)
        bet = sb("bet", [P, 1], F32)

        with ExitStack() as l0:
            wq = [sb(f"wq_{k}", [P, LOG], F16, l0) for k in "hl"]
            wv = [sb(f"wv_{k}", [P, K2 * C], F16, l0) for k in "hl"]
            wp = sb("wp", [P, 2, C], F32, l0)
            exp_scale = sb("exp_scale", [P, 1], F32, l0)
            first_row = sb("first_row", [P, IT], F32, l0)
            last_row = sb("last_row", [P, IT], F32, l0)
            band = sb("band", [P, 4, 2 * TILES, WIN * WC], F16, l0)
            vt = sb("vt", [P, 4, 2 * TILES, 256], F16, l0)
            xn = [sb(f"xn_{k}", [P, RING, W + 2], F16, l0) for k in "hl"]
            carry = sb("carry", [P, 2, 2, 256], F32, l0)

            with ExitStack() as c:
                wq_in = sb("wq_in", [P, 3, C], F32, c)
                wv_in = sb("wv_in", [P, K2, C], F32, c)
                wp_in = sb("wp_in", [P, C], F32, c)
                wp_dup = sb("wp_dup", [P, 2, 2, 2, HD], F32, c)
                wb_in = sb("wb_in", [P, K2, C], F32, c)
                wb_ge = sb("wb_ge", [P, K2, C], F32, c)
                wb_abs = sb("wb_abs", [P, K2, C], F32, c)
                wtf = sb("wtf", [P, LOG], F32, c)
                wvf = sb("wvf", [P, K2 * C], F32, c)
                top = sb("top", [P, 2], F32, c)
                top_row = sb("top_row", [2, 1], F32, c)
                top_pow = sb("top_pow", [2, 1], U32, c)
                diag = sb("diag", [2, 2], F32, c)
                pw = sb("pw", [P, 2], F32, c)
                ipw = sb("ipw", [P, 2], F32, c)
                zero = sb("zero", [8, 2 * K2 * 256], F16, c)
                twos = sb("twos", [P, P], F16, c)
                ps = [psum(f"pw{k}", [P, 512], F32, c) for k in range(7)]
                s_ld = [sem(f"a_ld{k}", c) for k in range(4)]
                s_gb = sem("a_gb", c)
                s_cst = sem("a_cst", c)
                s_cst2 = sem("a_cst2", c)
                s_zero = sem("a_zero", c)
                s_pad = sem("a_pad", c)
                s_dup = sem("a_dup", c)
                s_top = sem("a_top", c)
                s_topt = sem("a_topt", c)
                s_chain = sem("a_chain", c)
                s_diag = sem("a_diag", c)
                s_pw = sem("a_pw", c)
                s_tq = sem("a_tq", c)
                s_tv = sem("a_tv", c)
                s_tp = sem("a_tp", c)
                s_f = sem("a_f", c)
                s_hi = sem("a_hi", c)
                s_bin = sem("a_bin", c)
                s_bins = sem("a_bins", c)
                s_done = sem("a_done", c)
                with nc.Block() as block:
                    @block.sync
                    def _(sp):
                        sp.dma_start(wq_in[0:108], w_qkv.rearrange("(a p) c -> p a c", p=108)).then_inc(s_ld[0], 16)
                        sp.dma_start(wv_in[:], w_v.rearrange("q i j -> i q j")).then_inc(s_ld[1], 16)
                        sp.dma_start(wp_in[:], w_proj).then_inc(s_ld[2], 16)
                        sp.dma_start(wb_in[:], w_bin.rearrange("a b i o -> i (a b) o")).then_inc(s_ld[3], 16)
                        sp.dma_start(gam[:], gamma.rearrange("(c a) -> c a", a=1)).then_inc(s_gb, 16)
                        sp.dma_start(bet[:], beta.rearrange("(c a) -> c a", a=1)).then_inc(s_gb, 16)
                        sp.wait_ge(s_zero, 1)
                        sp.dma_start(v_d.rearrange("s r n c -> (s r) n c")[:, W:WP, :],
                                     zero[:].rearrange("p (n c) -> p n c", n=2)).then_inc(s_pad, 16)
                        sp.dma_start(a_d.rearrange("s r n c -> (s r) n c")[:, W:WP, :],
                                     zero[:, 0:4 * LOG].rearrange("p (n c) -> p n c", n=2)).then_inc(s_pad, 16)
                        sp.wait_ge(s_pad, 32)
                        sp.wait_ge(s_gb, 32)

                    @block.gpsimd
                    def _(pool):
                        pool.memset(zero[:], 0.0).then_inc(s_zero, 1)
                        pool.memset(ident[:], 0.0).then_inc(s_cst2, 1)
                        pool.memset(ones[:], 1.0).then_inc(s_cst, 1)
                        pool.memset(group[:], 1.0).then_inc(s_cst2, 1)
                        pool.memset(ones16[:], 1.0).then_inc(s_cst, 1)
                        pool.memset(twos[:], 1.0).then_inc(s_cst, 1)
                        pool.wait_ge(s_cst2, 2)
                        pool.affine_select(out=ident[:], in_=ident[:], compare_op=ALU.not_equal, fill=1.0, base=0,
                                           pattern=[[-1, P]], channel_multiplier=1).then_inc(s_cst, 1)
                        gv = group[:].rearrange("p (g e) -> p g e", e=4)
                        pool.affine_select(out=gv, in_=gv, compare_op=ALU.is_ge, fill=0.0, base=0,
                                           pattern=[[-4, 32], [0, 4]], channel_multiplier=1).then_inc(s_cst2, 1)
                        pool.wait_ge(s_cst2, 3)
                        pool.affine_select(out=gv, in_=gv, compare_op=ALU.is_ge, fill=0.0, base=3,
                                           pattern=[[4, 32], [0, 4]], channel_multiplier=-1).then_inc(s_cst, 1)
                        pool.memset(xn[0][:], 0.0).then_inc(s_cst, 1)
                        pool.memset(xn[1][:], 0.0).then_inc(s_cst, 1)
                        pool.memset(carry[:], 0.0).then_inc(s_cst, 1)
                        pool.memset(acc_sum[:], 0.0).then_inc(s_cst, 1)
                        pool.memset(acc_sq[:], 0.0).then_inc(s_cst, 1)
                        pool.memset(band[:, 0:2].bitcast(U32), 0).then_inc(s_cst, 1)
                        pool.wait_ge(s_cst, 11)

                    @block.vector
                    def _(dve):
                        dve.memset(top[:], 0.0).then_inc(s_chain, 1)
                        dve.memset(first_row[:], 1.0).then_inc(s_chain, 1)
                        dve.memset(last_row[:], 1.0).then_inc(s_chain, 1)
                        dve.wait_ge(s_chain, 3)
                        dve.memset(first_row[:].rearrange("p (b i) -> p b i", b=B)[:, :, 0:1], 0.0).then_inc(s_chain, 1)
                        dve.memset(last_row[:].rearrange("p (b i) -> p b i", b=B)[:, :, IPI - 1:IPI], 0.0).then_inc(s_chain, 1)
                        dve.memset(band[:, 2:4].bitcast(U32), 0).then_inc(s_chain, 1)
                        dve.wait_ge(s_ld[0], 16)
                        dve.tensor_reduce(top[0:108, 0:1], wq_in[0:108], AX.XY, ALU.max, apply_absolute_value=True).then_inc(s_top, 1)
                        dve.wait_ge(s_ld[1], 16)
                        dve.tensor_reduce(top[:, 1:2], wv_in[:], AX.XY, ALU.max, apply_absolute_value=True).then_inc(s_top, 1)
                        dve.wait_ge(s_topt, 1)
                        dve.tensor_reduce(top_row[:], ps[0][0:2, 0:P], AX.X, ALU.max).then_inc(s_chain, 1)
                        dve.wait_ge(s_chain, 7)
                        dve.tensor_scalar(top_row[:], top_row[:], 1e-30, None, ALU.max).then_inc(s_chain, 1)
                        dve.wait_ge(s_chain, 8)
                        dve.tensor_scalar(top_pow[:], top_row[:].bitcast(U32), 0x7F800000, None, ALU.bitwise_and).then_inc(s_chain, 1)
                        dve.wait_ge(s_chain, 9)
                        dve.wait_ge(s_cst, 4)
                        dve.tensor_scalar(diag[:], ident[0:2, 0:2], top_pow[:].bitcast(F32), None, ALU.mult).then_inc(s_diag, 1)
                        dve.wait_ge(s_pw, 1)
                        dve.tensor_copy(pw[:], ps[1][:, 0:2]).then_inc(s_chain, 1)
                        dve.wait_ge(s_chain, 10)
                        dve.reciprocal(ipw[:], pw[:]).then_inc(s_chain, 1)
                        dve.tensor_scalar(exp_scale[:], pw[:, 0:1], float(HD) ** -0.5, None, ALU.mult).then_inc(s_chain, 1)
                        dve.wait_ge(s_chain, 12)
                        dve.wait_ge(s_tq, 1)
                        lv = ps[2][:, 0:LOG].rearrange("p (h i j q) -> p q j i h", h=HEADS, i=3, j=3)
                        for q in range(K2):
                            dve.tensor_scalar(wtf[:, q * NPH:(q + 1) * NPH].rearrange("p (j i h) -> p j i h", j=3, i=3),
                                              lv[:, q], ipw[:, 0:1], None, ALU.mult).then_inc(s_f, 1)
                        dve.wait_ge(s_tv, 1)
                        for g in range(3):
                            dve.tensor_scalar(wvf[:, g * 384:(g + 1) * 384], ps[3 + g][:, 0:384], ipw[:, 1:2], None,
                                              ALU.mult).then_inc(s_f, 1)
                        dve.wait_ge(s_tp, 1)
                        dve.tensor_scalar(wp[:].rearrange("p a o -> p (a o)"), ps[6][:, 0:256], pw[:, 1:2], None, ALU.mult).then_inc(s_done, 1)
                        dve.wait_ge(s_hi, 2)
                        dve.tensor_tensor(wq[1][:], wtf[:], wq[0][:], ALU.subtract).then_inc(s_done, 1)
                        dve.tensor_tensor(wv[1][:], wvf[:], wv[0][:], ALU.subtract).then_inc(s_done, 1)
                        dve.wait_ge(s_ld[3], 16)
                        dve.tensor_scalar(wb_ge[:], wb_in[:], 0.0, 4.0, ALU.is_ge, ALU.mult).then_inc(s_chain, 1)
                        dve.wait_ge(s_chain, 13)
                        dve.tensor_scalar(wbin[:], wb_ge[:], -2.0, None, ALU.add).then_inc(s_bin, 1)
                        dve.wait_ge(s_bins, 1)
                        dve.tensor_scalar(neg_sum[:], ps[0][0:1, 256:384], -0.5, None, ALU.mult).then_inc(s_done, 1)
                        dve.wait_ge(s_bins, 2)
                        for r in range(4):
                            dve.tensor_scalar(wscale[:, r, :], ps[1][:, 256:384], 1.0 / (K2 * C), None, ALU.mult).then_inc(s_done, 1)
                        dve.wait_ge(s_done, 8)

                    @block.scalar
                    def _(act):
                        act.wait_ge(s_ld[2], 16)
                        for hl in range(2):
                            act.activation(wp_dup[:, :, :, hl, :].rearrange("o a h d -> o (a h) d"),
                                           wp_in[:].rearrange("o (h d) -> o h d", d=HD), ACT.Copy).then_inc(s_dup, 1)
                        act.wait_ge(s_ld[3], 16)
                        act.activation(wb_abs[:], wb_in[:], ACT.Abs).then_inc(s_bin, 1)
                        act.wait_ge(s_f, K2 + 3)
                        act.activation(wq[0][:], wtf[:], ACT.Copy).then_inc(s_hi, 1)
                        act.activation(wv[0][:], wvf[:], ACT.Copy).then_inc(s_hi, 1)

                    @block.tensor
                    def _(pe):
                        pe.wait_ge(s_cst, 5)
                        pe.wait_ge(s_top, 2)
                        pe.transpose(ps[0][0:2, 0:P], top[:], ident[:]).then_inc(s_topt, 1)
                        for a in range(3):
                            last = pe.transpose(ps[2][:, a * 108:(a + 1) * 108], wq_in[0:108, a, :], ident[0:108, 0:108])
                        last.then_inc(s_tq, 1)
                        for q in range(K2):
                            last = pe.transpose(ps[3 + q // 3][:, (q % 3) * C:(q % 3 + 1) * C], wv_in[:, q, :], ident[:])
                        last.then_inc(s_tv, 1)
                        pe.wait_ge(s_dup, 2)
                        for a in range(2):
                            last = pe.transpose(ps[6][:, a * C:(a + 1) * C],
                                                wp_dup[:, a].rearrange("o h l d -> o (h l d)"), ident[:])
                        last.then_inc(s_tp, 1)
                        pe.wait_ge(s_diag, 1)
                        pe.matmul(ps[1][:, 0:2], ones[0:2, :], diag[:], start=True, stop=True).then_inc(s_pw, 1)
                        pe.wait_ge(s_bin, 2)
                        for q in range(K2):
                            last = pe.matmul(ps[0][:, 256:384], twos[:], wbin[:, q, :], start=q == 0, stop=q == K2 - 1)
                        last.then_inc(s_bins, 1)
                        for q in range(K2):
                            last = pe.matmul(ps[1][:, 256:384], ones[:], wb_abs[:, q, :], start=q == 0, stop=q == K2 - 1)
                        last.then_inc(s_bins, 1)

            with ExitStack() as c:
                xc = sb("xc", [P, 4, CH, C], F32, c)
                xsq = sb("xsq", [P, 2, CH, C], F32, c)
                part = sb("part", [P, NCH, C], F32, c)
                sums = sb("sums", [P, B, C], F32, c)
                sqs = sb("sqs", [P, B, C], F32, c)
                ps_sum = psum("ps_sum", [P, 512], F32, c)
                s_x = [sem(f"b_x{k}", c) for k in range(4)]
                s_sum = sem("b_sum", c)
                s_sq = sem("b_sq", c)
                s_part = sem("b_part", c)
                s_img = sem("b_img", c)
                s_isq = sem("b_isq", c)
                with nc.Block() as block:
                    @block.sync
                    def _(sp):
                        with sp.Fori(0, B) as b:
                            for k in range(NCH):
                                if k >= 4:
                                    sp.wait_ge(s_sum, NCH * b + k - 3)
                                    sp.wait_ge(s_sq, NCH * b + k - 3)
                                else:
                                    sp.wait_ge(s_sum, NCH * b)
                                    sp.wait_ge(s_sq, NCH * b)
                                sp.dma_start(xc[:, k % 4].rearrange("p n c -> p (n c)"),
                                             xchunks[bass.ds(b * NCH + k, 1)].rearrange("a p n -> (a p) n")).then_inc(s_x[k % 4], 16)

                    @block.tensor
                    def _(pe):
                        with pe.Fori(0, B) as b:
                            for k in range(NCH):
                                pe.wait_ge(s_x[k % 4], 16 * ((b * NCH + k) // 4 + 1))
                                if k == 0:
                                    pe.wait_ge(s_img, b)
                                for g in range(CH // 4):
                                    last = pe.matmul(ps_sum[:], ones[:], xc[:, k % 4, 4 * g:4 * g + 4, :].rearrange("p r c -> p (r c)"),
                                                     start=k == 0 and g == 0, stop=k == NCH - 1 and g == CH // 4 - 1)
                                last.then_inc(s_sum, 1)

                    @block.scalar
                    def _(act):
                        with act.Fori(0, B) as b:
                            for k in range(NCH):
                                act.wait_ge(s_x[k % 4], 16 * ((b * NCH + k) // 4 + 1))
                                if k >= 2:
                                    act.wait_ge(s_part, NCH * b + k - 1)
                                else:
                                    act.wait_ge(s_part, NCH * b)
                                act.activation(xsq[:, k % 2], xc[:, k % 4], ACT.Square).then_inc(s_sq, 1)

                    @block.vector
                    def _(dve):
                        with dve.Fori(0, B) as b:
                            dve.wait_ge(s_isq, b)
                            for k in range(NCH):
                                dve.wait_ge(s_sq, NCH * b + k + 1)
                                dve.tensor_reduce(part[:, k, :], xsq[:, k % 2].rearrange("p r c -> p c r"), AX.X, ALU.add).then_inc(s_part, 1)
                            dve.wait_ge(s_sum, NCH * (b + 1))
                            dve.tensor_reduce(sums[:, bass.ds(b, 1), :].rearrange("p a c -> p (a c)"), ps_sum[:].rearrange("p (r c) -> p c r", c=C), AX.X, ALU.add).then_inc(s_img, 1)
                            dve.wait_ge(s_part, NCH * (b + 1))
                            dve.tensor_reduce(sqs[:, bass.ds(b, 1), :].rearrange("p a c -> p (a c)"), part[:].rearrange("p k c -> p c k"), AX.X, ALU.add).then_inc(s_isq, 1)

                norm_params(nc, "c", B, NPIX, 1.0, EPS_GN, [sums[0:1]], [sqs[:]], ones, group,
                            gn_scale[:], gn_bias[:])

            with ExitStack() as c:
                x_in = sb("x_in", [P, 4, 2, C], F32, c)
                x_res = sb("x_res", [P, 4, 2, C], F32, c)
                x1_s = sb("x1_s", [P, 4, 2, C], F32, c)
                x1_sq = sb("x1_sq", [P, 256], F32, c)
                xf = sb("xf", [P, 2, 2, W], F32, c)
                v_s = sb("v_s", [P, 2, 2, K2 * 256], F16, c)
                a_s = sb("a_s", [P, 2, 2, LOG, 2], F16, c)
                e = sb("e", [P, 2, 2, LOG], F32, c)
                an = sb("an", [P, 2, 2, LOG], F32, c)
                gn_now = sb("gn_now", [P, 2], F32, c)
                mx = sb("mx", [P, 2, NPH], F32, c)
                sm = sb("sm", [P, 2, NPH], F32, c)
                ri = sb("ri", [P, 2, 2, NPH], F32, c)
                y_s = sb("y_s", [P, 2, 2, 256], F32, c)
                ps_y = [psum(f"ps_y{k}", [P, 2, 512], F32, c) for k in range(2)]
                ps_v = [psum(f"ps_v{k}", [P, 512], F32, c) for k in range(2)]
                ps_l = psum("ps_l", [P, 512], F32, c)
                ps_m = psum("ps_m", [P, 512], F32, c)
                s_xl = [sem(f"x_loaded{k}", c) for k in range(4)]
                s_xr = [sem(f"xres_loaded{k}", c) for k in range(4)]
                s_wv = [sem(f"v_written{k}", c) for k in range(4)]
                s_wa = [sem(f"a_written{k}", c) for k in range(4)]
                s_rd = [sem(f"band_loaded{k}", c) for k in range(4)]
                s_st = [sem(f"x1_stored{k}", c) for k in range(4)]
                t_done = sem("t_done", c)
                v_done = sem("v_done", c)
                l_done = sem("l_done", c)
                y_done = sem("y_done", c)
                z_done = sem("z_done", c)
                e_done = sem("e_done", c)
                xhi_done = sem("xhi_done", c)
                vhi_done = sem("vhi_done", c)
                carry_done = sem("carry_done", c)
                ahi_done = sem("ahi_done", c)
                g_done = sem("g_done", c)
                xf_done = sem("xf_done", c)
                vlo_done = sem("vlo_done", c)
                mx_done = sem("mx_done", c)
                d_done = sem("d_done", c)
                sm_done = sem("sm_done", c)
                r_raw = sem("r_raw", c)
                r_done = sem("r_done", c)
                fold_done = sem("fold_done", c)
                x1_done = sem("x1_done", c)
                an_done = sem("an_done", c)
                xlo_done = sem("xlo_done", c)
                alo_done = sem("alo_done", c)
                sq_done = sem("sq_done", c)
                stat_done = sem("stat_done", c)

                FRONT, BACK = (-1, 0, 1, 2), (IT - 1, IT, IT + 1)

                def run_steps(eng, step):
                    for i in FRONT:
                        for u in range(4):
                            step(i, u)
                    if IT - 1 > 3:
                        with eng.Fori(3, IT - 1) as i:
                            for u in range(4):
                                step(i, u)
                    for i in BACK:
                        for u in range(4):
                            step(i, u)

                def least(i, count):
                    return min(count, NP) if isinstance(i, int) else count

                with nc.Block() as block:
                    @block.sync
                    def _(sp):
                        def load_x(i, u, d):
                            slot, it = place(i, u, d)
                            p = 4 * i + u + d
                            after(sp, t_done, p - 3)
                            sp.dma_start(x_in[:, slot], xr_v[bass.ds(2 * p, 2)].rearrange("r w c -> w r c")).then_inc(s_xl[slot], 16)

                        def step(i, u):
                            s = 4 * i + u
                            if valid(i, u, 4):
                                load_x(i, u, 4)
                            if valid(i, u, -4):
                                slot, it = place(i, u, -4)
                                after(sp, x1_done, s - 7)
                                sp.dma_start(x_res[:, slot], xr_v[bass.ds(2 * s - 8, 2)].rearrange("r w c -> w r c")).then_inc(s_xr[slot], 16)
                            if valid(i, u, -2):
                                slot, it = place(i, u, -2)
                                if isinstance(i, int):
                                    after(sp, y_done, s - 5)
                                sp.wait_ge(s_wv[slot], 16 * (it + 1))
                                sp.wait_ge(s_wa[slot], 16 * (it + 1))
                                sp.dma_start(vt[0:KT, slot], v_d[slot].rearrange("r n c -> (r n c)").rearrange("(t k c) -> k t c", k=KT, c=256)).then_inc(s_rd[slot], 16)
                                av = a_d[slot].rearrange("r n c -> (r n c)").rearrange("(t j q c) -> j q t c", j=JT, q=K2, c=2 * NPH)
                                for j in range(JT):
                                    sp.dma_start(band[K2 * j:K2 * (j + 1), slot, :, WC * j:WC * j + 2 * NPH], av[j]).then_inc(s_rd[slot], 16)
                            if valid(i, u, -1):
                                slot, it = place(i, u, -1)
                                after(sp, s_rd[slot], 16 * 14 * it) if isinstance(i, int) else None
                                sp.wait_ge(alo_done, s)
                                sp.dma_start(a_d[slot].rearrange("r n c -> n r c")[0:W], a_s[:, (u - 1) % 2].rearrange("p r l k -> p r (l k)")).then_inc(s_wa[slot], 16)
                            if valid(i, u, -6):
                                slot, it = place(i, u, -6)
                                sp.wait_ge(x1_done, s - 5)
                                sp.dma_start(x1_d[bass.ds(2 * s - 12, 2)].rearrange("r w c -> w r c"), x1_s[:, slot]).then_inc(s_st[slot], 16)

                        run_steps(sp, step)
                        for k in range(4):
                            sp.wait_ge(s_st[k], 16 * IT)

                    @block.tensor
                    def _(pe):
                        def transposes(i, u):
                            slot, it = place(i, u, 2)
                            s = 4 * i + u
                            pe.wait_ge(s_xl[slot], 16 * (it + 1))
                            after(pe, xf_done, s + 2)
                            after(pe, x1_done, s - 6)
                            for r in range(2):
                                last = pe.transpose(ps_m[:, 256 + r * W:256 + (r + 1) * W], x_in[:, slot, r, :], ident[:])
                            last.then_inc(t_done, 1)

                        def values(i, u, g):
                            s = 4 * i + u
                            r, di = g // 3, g % 3
                            after(pe, vlo_done, 6 * s + g - 1)
                            if g % 3 == 0:
                                pe.wait_ge(xlo_done, least(i, s + 1 + r))
                            row = (2 * u + r + di - 1) % RING
                            for dj in range(3):
                                q = 3 * di + dj
                                for n, (a, b) in enumerate(((0, 0), (0, 1), (1, 0))):
                                    last = pe.matmul(ps_v[g % 2][:, dj * C:(dj + 1) * C], xn[a][:, row, dj:dj + W],
                                                     wv[b][:, q * C:(q + 1) * C], start=n == 0, stop=n == 2)
                            last.then_inc(v_done, 1)

                        def logits(i, u, r):
                            s = 4 * i + u
                            after(pe, d_done, 2 * s + r)
                            row = (2 * u + r) % RING
                            for n, (a, b) in enumerate(((0, 0), (0, 1), (1, 0))):
                                last = pe.matmul(ps_l[:, 0:LOG], xn[a][:, row, 1:1 + W], wq[b][:], start=n == 0, stop=n == 2)
                            last.then_inc(l_done, 1)

                        def bands(i, u, part):
                            slot, it = place(i, u, -4)
                            s = 4 * i + u
                            y = ps_y[u % 2]
                            if part == 0:
                                pe.wait_ge(s_rd[slot], 16 * 14 * (it + 1))
                                after(pe, carry_done, s - 5)
                            for tile in range(20 * part // 8, 20 * (part + 1) // 8):
                                r, t = tile // TILES, tile % TILES
                                lo = 1 if t == 0 else 0
                                hi = min(WIN, W + 1 - JT * t)
                                col = JT * t - 1 + lo
                                win = band[0:KT, slot, tile, :].rearrange("k (m i h l) -> k h l i m", i=3, h=HEADS, l=2)
                                for h in range(HEADS):
                                    for l in range(2):
                                        o = y[64 * (h % 2):64 * (h % 2) + 64, h // 2, :].rearrange("p (s m) -> p s m", m=W)
                                        last = pe.matmul(o[:, r:r + 3, col:col + hi - lo],
                                                         vt[0:KT, slot, tile, 64 * h:64 * h + 64],
                                                         win[:, h, l, :, lo:hi], start=tile == 0 and l == 0,
                                                         stop=tile == 2 * TILES - 1 and l == 1, skip_group_check=True)
                            if part == 7:
                                last.then_inc(y_done, 1)

                        def project(i, u):
                            s = 4 * i + u
                            pe.wait_ge(fold_done, s - 4)
                            pe.wait_ge(xf_done, least(i, s + 3))
                            after(pe, x1_done, s - 6)
                            q0, q1 = u % 2, (u + 1) % 2
                            for r, (slot, off) in enumerate(((q0, W), (q1, 0))):
                                for a in range(2):
                                    last = pe.matmul(ps_m[:, r * C:(r + 1) * C], y_s[:, slot, a, off:off + W], wp[:, a, :],
                                                     start=a == 0, stop=a == 1)
                            last.then_inc(z_done, 1)

                        def step(i, u):
                            if valid(i, u, 2):
                                transposes(i, u)
                            for n in range(8):
                                if valid(i, u, 0):
                                    if n % 4 < 3:
                                        values(i, u, 3 * (n // 4) + n % 4)
                                    else:
                                        logits(i, u, n // 4)
                                if n == 4 and valid(i, u, -6):
                                    project(i, u)
                                if valid(i, u, -4):
                                    bands(i, u, n)

                        run_steps(pe, step)

                    @block.scalar
                    def _(act):
                        def step(i, u):
                            s = 4 * i + u
                            if valid(i, u, -1):
                                act.wait_ge(d_done, 2 * s)
                                ep = e[:, (u - 1) % 2].rearrange("p r k -> p (r k)")
                                act.activation(ep, ep, ACT.Exp, scale=exp_scale[:, 0:1]).then_inc(e_done, 1)
                            if valid(i, u, 2):
                                slot, it = place(i, u, 2)
                                act.wait_ge(g_done, 2 * it + 2)
                                after(act, v_done, 6 * s)
                                act.wait_ge(t_done, s + 3)
                                act.activation(xn[0][:, 2 * slot:2 * slot + 2, 1:1 + W], ps_m[:, 256:512].rearrange("p (r w) -> p r w", r=2),
                                               ACT.Identity, bias=gn_now[:, 1:2], scale=gn_now[:, 0:1]).then_inc(xhi_done, 1)
                            for g in range(6):
                                if g == 1 and valid(i, u, -1):
                                    slot, it = place(i, u, -1)
                                    act.wait_ge(vlo_done, 6 * s)
                                    after(act, s_rd[slot], 16 * 14 * it)
                                    act.dma_start(v_d[slot].rearrange("r n c -> n r c")[0:W], v_s[:, (u - 1) % 2]).then_inc(s_wv[slot], 16)
                                if g == 1 and valid(i, u, -5):
                                    act.wait_ge(fold_done, s - 4)
                                    act.activation(carry[:, (u - 5) % 2], ps_y[(u - 5) % 2][:, :, 256:512], ACT.Copy).then_inc(carry_done, 1)
                                if g == 4 and valid(i, u, -1):
                                    slot, it = place(i, u, -3)
                                    act.wait_ge(an_done, s)
                                    if valid(i, u, -3):
                                        act.wait_ge(s_wa[slot], 16 * (it + 1))
                                    act.activation(a_s[:, (u - 1) % 2, :, :, 0], an[:, (u - 1) % 2], ACT.Copy).then_inc(ahi_done, 1)
                                if valid(i, u, 0):
                                    slot, it = place(i, u, -2)
                                    act.wait_ge(v_done, 6 * s + g + 1)
                                    if g == 0 and valid(i, u, -2):
                                        act.wait_ge(s_wv[slot], 16 * (it + 1))
                                    vp = v_s[:, u % 2, g // 3, 768 * (g % 3):768 * (g % 3 + 1)].rearrange("p (h l d) -> p h l d", l=2, d=HD)
                                    act.activation(vp[:, :, 0, :], ps_v[g % 2][:, 0:384].rearrange("p (h d) -> p h d", d=HD),
                                                   ACT.Copy).then_inc(vhi_done, 1)

                        run_steps(act, step)

                    @block.vector
                    def _(dve):
                        def softmax_top(i, u, r):
                            s = 4 * i + u
                            dve.wait_ge(l_done, 2 * s + r + 1)
                            after(dve, d_done, 2 * s + r - 1)
                            if r == 0:
                                after(dve, an_done, s - 1)
                            lv = ps_l[:, 0:LOG].rearrange("p (q k) -> p q k", q=K2)
                            dve.tensor_reduce(mx[:, r, :], lv.rearrange("p q k -> p k q"), AX.X, ALU.max).then_inc(mx_done, 1)
                            dve.wait_ge(mx_done, 2 * s + r + 1)
                            dve.tensor_tensor(e[:, u % 2, r, :].rearrange("p (q k) -> p q k", q=K2), lv,
                                              mx[:, r, :].unsqueeze(1).to_broadcast([P, K2, NPH]), ALU.subtract).then_inc(d_done, 1)

                        def softmax_sum(i, u):
                            s = 4 * i + u
                            v = (u - 1) % 2
                            dve.wait_ge(e_done, s)
                            after(dve, an_done, s - 2)
                            dve.tensor_reduce(sm[:], e[:, v].rearrange("p r (q k) -> p r k q", q=K2), AX.X, ALU.add).then_inc(sm_done, 1)
                            dve.wait_ge(sm_done, s)
                            edge = u in (0, 1)
                            dve.reciprocal(ri[:, v], sm[:]).then_inc(r_raw if edge else r_done, 1)
                            if edge:
                                it = i if u == 1 else i - 1
                                row, di, keep = (0, 0, first_row) if u == 1 else (1, 2, last_row)
                                ev = e[:, v, row, 3 * di * NPH:3 * (di + 1) * NPH]
                                dve.tensor_scalar(ev, ev, keep[:, bass.ds(it, 1)], None, ALU.mult).then_inc(r_raw, 1)
                                dve.wait_ge(r_raw, 4 * it + (2 if u == 1 else 4))
                                rv = ri[:, v, row, :].rearrange("p (j i h) -> p j i h", j=3, i=3)[:, :, di, :]
                                dve.tensor_scalar(rv, rv, keep[:, bass.ds(it, 1)], None, ALU.mult).then_inc(r_done, 1)

                        def step(i, u):
                            s = 4 * i + u
                            if valid(i, u, -5):
                                dve.wait_ge(y_done, s - 4)
                                after(dve, carry_done, s - 5)
                                after(dve, z_done, s - 6)
                                dve.tensor_tensor(y_s[:, (u - 5) % 2], ps_y[(u - 5) % 2][:, :, 0:256], carry[:, (u - 6) % 2],
                                                  ALU.add).then_inc(fold_done, 1)
                            elif isinstance(i, int) and s - 5 == NP:
                                dve.wait_ge(carry_done, NP)
                                dve.wait_ge(z_done, NP - 1)
                                dve.tensor_copy(y_s[:, NP % 2, :, 0:W], carry[:, (NP - 1) % 2, :, 0:W]).then_inc(fold_done, 1)
                            if valid(i, u, 2):
                                slot, it = place(i, u, 2)
                                if u == 2:
                                    img = it // IPI
                                    for k, par in enumerate((gn_scale, gn_bias)):
                                        dve.tensor_scalar(gn_now[:, k:k + 1], par[:, bass.ds(img, 1)], 1.0, None, ALU.mult).then_inc(g_done, 1)
                                    dve.wait_ge(g_done, 2 * it + 2)
                                dve.wait_ge(xhi_done, s + 3)
                                after(dve, xlo_done, s + 1)
                                dve.tensor_scalar(xf[:, u % 2].rearrange("p r w -> p (r w)"), ps_m[:, 256:512],
                                                  gn_now[:, 0:1], gn_now[:, 1:2], ALU.mult, ALU.add).then_inc(xf_done, 1)
                            for g in range(6):
                                if g == 1 and valid(i, u, -1):
                                    softmax_sum(i, u)
                                if g == 3 and valid(i, u, 0):
                                    softmax_top(i, u, 0)
                                if g == 4 and valid(i, u, -6):
                                    slot, it = place(i, u, -6)
                                    dve.wait_ge(z_done, s - 5)
                                    dve.wait_ge(s_xr[slot], 16 * (it + 1))
                                    after(dve, s_st[slot], 16 * it)
                                    after(dve, stat_done, s - 9)
                                    dve.tensor_tensor(x1_s[:, slot].rearrange("p r c -> p (r c)"), ps_m[:, 0:256],
                                                      x_res[:, slot].rearrange("p r c -> p (r c)"), ALU.add).then_inc(x1_done, 1)
                                if valid(i, u, 0):
                                    dve.wait_ge(vhi_done, 6 * s + g + 1)
                                    vp = v_s[:, u % 2, g // 3, 768 * (g % 3):768 * (g % 3 + 1)].rearrange("p (h l d) -> p h l d", l=2, d=HD)
                                    dve.tensor_tensor(vp[:, :, 1, :], ps_v[g % 2][:, 0:384].rearrange("p (h d) -> p h d", d=HD),
                                                      vp[:, :, 0, :], ALU.subtract).then_inc(vlo_done, 1)
                            if valid(i, u, 0):
                                softmax_top(i, u, 1)

                        run_steps(dve, step)

                    @block.gpsimd
                    def _(pool):
                        def step(i, u):
                            s = 4 * i + u
                            v = (u - 1) % 2
                            if valid(i, u, -1):
                                pool.wait_ge(r_done, s)
                                after(pool, ahi_done, s - 2)
                                after(pool, alo_done, s - 2)
                                pool.tensor_tensor(an[:, v].rearrange("p r (q k) -> p r q k", q=K2),
                                                   e[:, v].rearrange("p r (q k) -> p r q k", q=K2),
                                                   ri[:, v].unsqueeze(2).to_broadcast([P, 2, K2, NPH]),
                                                   ALU.mult).then_inc(an_done, 1)
                            if valid(i, u, 2):
                                slot, it = place(i, u, 2)
                                pool.wait_ge(xf_done, s + 3)
                                after(pool, v_done, 6 * s)
                                pool.tensor_tensor(xn[1][:, 2 * slot:2 * slot + 2, 1:1 + W], xf[:, u % 2],
                                                   xn[0][:, 2 * slot:2 * slot + 2, 1:1 + W], ALU.subtract).then_inc(xlo_done, 1)
                            if valid(i, u, -6):
                                slot, it = place(i, u, -6)
                                img = it // IPI
                                pool.wait_ge(x1_done, s - 5)
                                after(pool, stat_done, s - 6)
                                x1p = x1_s[:, slot].rearrange("p r c -> p (r c)")
                                sp_, qp = (t[:, bass.ds(img, 1), :].rearrange("p a c -> p (a c)") for t in (acc_sum, acc_sq))
                                pool.tensor_tensor(x1_sq[:], x1p, x1p, ALU.mult).then_inc(sq_done, 1)
                                pool.tensor_tensor(sp_, sp_, x1p, ALU.add).then_inc(sq_done, 1)
                                pool.wait_ge(sq_done, 2 * (s - 5))
                            if valid(i, u, -1):
                                pool.wait_ge(ahi_done, s)
                                pool.tensor_tensor(a_s[:, v, :, :, 1], an[:, v], a_s[:, v, :, :, 0], ALU.subtract).then_inc(alo_done, 1)
                            if valid(i, u, -6):
                                pool.tensor_tensor(qp, qp, x1_sq[:], ALU.add).then_inc(stat_done, 1)

                        run_steps(pool, step)

        bin_a = sb("bin_a", [P, B], F32)
        bin_t = sb("bin_t", [P, B], F32)
        norm_params(nc, "d", B, NPIX, float(H * W), EPS_GN, [acc_sum[:, :, 0:C], acc_sum[:, :, C:2 * C]],
                    [acc_sq[:, :, 0:C], acc_sq[:, :, C:2 * C]], ones, group, gn_scale[:], gn_bias[:],
                    (gam[:], bet[:], EPS_BN, bin_a[:], bin_t[:]))

        NG = ROWS // 4
        ITG = NG // 4
        with ExitStack() as c:
            first = sb("first", [P, ITG], F32, c)
            final = sb("final", [P, ITG], F32, c)
            x1 = sb("x1", [P, 4, 4, C], F32, c)
            xb = sb("xb", [P, 16, W + 2], F16, c)
            above = sb("above", [P, W + 2], F16, c)
            below = sb("below", [P, W + 2], F16, c)
            conv = sb("conv", [P, 2, 4 * C], F32, c)
            o_s = sb("o_s", [P, 4, 4, C], F32, c)
            ps_t = [psum(f"ps_t{k}", [P, 512], F32, c) for k in range(2)]
            ps_c = [psum(f"ps_c{k}", [P, 512], F32, c) for k in range(2)]
            s_init = sem("init", c)
            s_x1 = [sem(f"x1_in{k}", c) for k in range(4)]
            s_out = [sem(f"out_stored{k}", c) for k in range(4)]
            tt_done = sem("tt_done", c)
            b_done = sem("b_done", c)
            h_done = sem("h_done", c)
            c_done = sem("c_done", c)
            m_done = sem("m_done", c)
            o_done = sem("o_done", c)

            def run_groups(eng, step):
                for i in (-1, 0):
                    for u in range(4):
                        step(i, u)
                if ITG > 2:
                    with eng.Fori(1, ITG - 1) as i:
                        for u in range(4):
                            step(i, u)
                for i in (ITG - 1, ITG):
                    for u in range(4):
                        step(i, u)

            def there(i, u, d):
                return not isinstance(i, int) or 0 <= 4 * i + u + d < NG

            with nc.Block() as block:
                @block.sync
                def _(sp):
                    def step(i, u):
                        g = 4 * i + u
                        if there(i, u, 4):
                            after(sp, o_done, g + 1)
                            sp.dma_start(x1[:, u], x1_d[bass.ds(4 * g + 16, 4)].rearrange("r w c -> w r c")).then_inc(s_x1[u], 16)
                        if there(i, u, -1):
                            sp.wait_ge(o_done, g)
                            sp.dma_start(out_v[bass.ds(4 * g - 4, 4)].rearrange("r w c -> w r c"), o_s[:, (u - 1) % 4]).then_inc(s_out[(u - 1) % 4], 16)

                    run_groups(sp, step)
                    for k in range(4):
                        sp.wait_ge(s_out[k], 16 * ITG)

                @block.tensor
                def _(pe):
                    pe.wait_ge(s_init, 5)

                    def step(i, u):
                        g = 4 * i + u
                        if there(i, u, 2):
                            slot, it = place(i, u, 2)
                            pe.wait_ge(s_x1[slot], 16 * (it + 1))
                            after(pe, b_done, g + 1)
                            for r in range(4):
                                last = pe.transpose(ps_t[u % 2][:, r * W:(r + 1) * W], x1[:, slot, r, :], ident[:])
                            last.then_inc(tt_done, 1)
                        if there(i, u, 0):
                            pe.wait_ge(b_done, min(g + 2, NG) if isinstance(i, int) else g + 2)
                            after(pe, m_done, g - 1)
                            if u == 0:
                                pe.wait_ge(h_done, 2 * i + 1)
                            if u == 3:
                                pe.wait_ge(h_done, 2 * i + 2)
                            for r in range(4):
                                row = 4 * u + r
                                o = ps_c[u % 2][:, r * C:(r + 1) * C]
                                pe.matmul(o, ones16[:], neg_sum[:], start=True, stop=False)
                                for di in range(3):
                                    src = above[:] if row + di == 0 else below[:] if row + di == 17 else xb[:, row + di - 1, :]
                                    for dj in range(3):
                                        last = pe.matmul(o, src[:, dj:dj + W], wbin[:, 3 * di + dj, :], start=False,
                                                         stop=di == 2 and dj == 2)
                            last.then_inc(c_done, 1)

                    run_groups(pe, step)

                @block.vector
                def _(dve):
                    dve.memset(first[:], 0.0).then_inc(s_init, 1)
                    dve.memset(final[:], 0.0).then_inc(s_init, 1)
                    dve.memset(xb[:], 1.0).then_inc(s_init, 1)
                    dve.wait_ge(s_init, 3)
                    per = H // 16
                    dve.memset(first[:].rearrange("p (b i) -> p b i", b=B)[:, :, 0:1], 1.0).then_inc(s_init, 1)
                    dve.memset(final[:].rearrange("p (b i) -> p b i", b=B)[:, :, per - 1:per], 1.0).then_inc(s_init, 1)

                    def step(i, u):
                        g = 4 * i + u
                        if there(i, u, 2):
                            slot, it = place(i, u, 2)
                            img = it // (H // 16)
                            dve.wait_ge(tt_done, g + 3)
                            after(dve, c_done, g)
                            after(dve, h_done, 2 * i + 1 if u >= 1 else 2 * i)
                            dve.tensor_scalar(xb[:, 4 * slot:4 * slot + 4, 1:1 + W], ps_t[u % 2][:].rearrange("p (r w) -> p r w", r=4),
                                              bin_a[:, bass.ds(img, 1)], bin_t[:, bass.ds(img, 1)], ALU.mult, ALU.is_ge).then_inc(b_done, 1)
                        if u == 3 and there(i, u, 1):
                            nxt = i + 1
                            after(dve, c_done, 4 * nxt - 3)
                            dve.wait_ge(b_done, 4 * nxt)
                            dve.tensor_scalar(above[:], xb[:, 15, :], first[:, bass.ds(nxt, 1)], None, ALU.max).then_inc(h_done, 1)
                        if u == 2 and there(i, u, 0):
                            after(dve, c_done, 4 * i)
                            dve.wait_ge(b_done, min(4 * i + 5, NG) if isinstance(i, int) else 4 * i + 5)
                            dve.tensor_scalar(below[:], xb[:, 0, :], final[:, bass.ds(i, 1)], None, ALU.max).then_inc(h_done, 1)
                        if there(i, u, 0):
                            dve.wait_ge(c_done, g + 1)
                            after(dve, o_done, g - 1)
                            dve.tensor_tensor(conv[:, u % 2], ps_c[u % 2][:], wscale[:].rearrange("p r c -> p (r c)"),
                                              ALU.mult).then_inc(m_done, 1)

                    run_groups(dve, step)

                @block.gpsimd
                def _(pool):
                    pool.wait_ge(s_init, 5)

                    def step(i, u):
                        g = 4 * i + u
                        if there(i, u, 0):
                            pool.wait_ge(m_done, g + 1)
                            after(pool, s_out[u], 16 * i)
                            pool.tensor_tensor(o_s[:, u].rearrange("p r c -> p (r c)"), conv[:, u % 2],
                                               x1[:, u].rearrange("p r c -> p (r c)"), ALU.add).then_inc(o_done, 1)

                    run_groups(pool, step)


_INS = ['x', 'L0_conv_w_qkv', 'L0_conv_w_v', 'L0_conv_w_proj', 'L1_conv_gamma', 'L1_conv_beta', 'L1_conv_W']


def kernel(**inputs):
    import numpy as _np
    import concourse.bacc as _bacc
    from concourse import mybir as _mybir
    from concourse.bass_utils import run_bass_kernel_spmd as _run

    nc = _bacc.Bacc("TRN2", target_bir_lowering=False, num_devices=1)
    arrays, args = {}, []
    for name in _INS:
        a = _np.ascontiguousarray(inputs[name])
        arrays[f"in_{name}"] = a
        args.append(nc.dram_tensor(f"in_{name}", a.shape, _mybir.dt.from_np(a.dtype), kind="ExternalInput").ap())
    out = nc.dram_tensor("out_0", inputs["x"].shape, F32, kind="ExternalOutput").ap()
    build_kernel(nc, *args, out)
    r = _run(nc, [arrays], core_ids=[0])
    return r.results[0]["out_0"]
```

```python
from contextlib import ExitStack

import concourse.bass as bass
from concourse import mybir

ALU = mybir.AluOpType
ACT = mybir.ActivationFunctionType
AX = mybir.AxisListType
F32 = mybir.dt.float32
F16 = mybir.dt.float16
U32 = mybir.dt.uint32

P = 128
W = 128
C = 128
HEADS = 4
HD = C // HEADS
K2 = 9
NPH = 3 * 3 * HEADS
LOG = K2 * NPH
JT = 13
KT = JT * K2
TILES = 10
WP = JT * TILES
WIN = JT + 2
DH = 3 * HEADS
AR = 4 * DH * 2
RING = 8
XR = 4
EPS_GN = 1e-5
EPS_BN = 1e-3


def norm_params(nc, tag, B, n_group, n_chan, eps, sums, sqs, ones, group, scale, bias, bn=None):
    with ExitStack() as c:
        def sb(name, shape):
            return c.enter_context(nc.sbuf_tensor(f"{tag}_{name}", shape, F32))

        cols, stat, tmp, root, q2, r2 = (sb(n, [P, 2 * B]) for n in ("cols", "stat", "tmp", "root", "q2", "r2"))
        one = sb("one", [P, 8])
        ps_c = c.enter_context(nc.psum_tensor(f"{tag}_ps_c", [P, 512], F32))
        ps_g = c.enter_context(nc.psum_tensor(f"{tag}_ps_g", [P, 512], F32))
        s_cols = c.enter_context(nc.semaphore(f"{tag}_cols_summed"))
        s_colc = c.enter_context(nc.semaphore(f"{tag}_cols_copied"))
        s_grp = c.enter_context(nc.semaphore(f"{tag}_groups_summed"))
        s_var = c.enter_context(nc.semaphore(f"{tag}_variance"))
        s_root = c.enter_context(nc.semaphore(f"{tag}_root"))
        s_chain = c.enter_context(nc.semaphore(f"{tag}_chain"))
        with nc.Block() as block:
            @block.tensor
            def _(pe):
                for k, parts in enumerate((sums, sqs)):
                    for b in range(B):
                        for n, t in enumerate(parts):
                            last = pe.matmul(ps_c[:, k * B + b:k * B + b + 1], t[:, b, :], ones[0:t.shape[0], 0:1],
                                             start=n == 0, stop=n == len(parts) - 1)
                last.then_inc(s_cols, 1)
                pe.wait_ge(s_colc, 1)
                pe.matmul(ps_g[:, 0:2 * B], group[:], cols[:], start=True, stop=True).then_inc(s_grp, 1)

            @block.scalar
            def _(act):
                act.wait_ge(s_var, 1)
                act.activation(root[:, 0:B], tmp[:, 0:B], ACT.Sqrt).then_inc(s_root, 1)
                if bn is not None:
                    act.wait_ge(s_var, 2)
                    act.activation(root[:, 0:1], one[:, 3:4], ACT.Sqrt).then_inc(s_root, 1)

            @block.vector
            def _(dve):
                chain = [0]

                def link(ins):
                    chain[0] += 1
                    ins.then_inc(s_chain, 1)
                    dve.wait_ge(s_chain, chain[0])

                def rsqrt(dst, v, n):
                    link(dve.reciprocal(dst, root[:, 0:n]))
                    link(dve.tensor_tensor(r2[:, 0:n], dst, dst, ALU.mult))
                    link(dve.tensor_tensor(r2[:, 0:n], r2[:, 0:n], v, ALU.mult))
                    link(dve.tensor_scalar(r2[:, 0:n], r2[:, 0:n], -0.5, 1.5, ALU.mult, ALU.add))
                    link(dve.tensor_tensor(dst, dst, r2[:, 0:n], ALU.mult))

                dve.wait_ge(s_cols, 1)
                dve.tensor_copy(cols[:], ps_c[:, 0:2 * B]).then_inc(s_colc, 1)
                dve.wait_ge(s_grp, 1)
                link(dve.tensor_scalar(stat[:], ps_g[:, 0:2 * B], 1.0 / n_group, None, ALU.mult))
                m = stat[:, 0:B]
                link(dve.tensor_tensor(tmp[:, B:2 * B], m, m, ALU.mult))
                link(dve.tensor_tensor(tmp[:, 0:B], stat[:, B:2 * B], tmp[:, B:2 * B], ALU.subtract))
                link(dve.tensor_scalar(tmp[:, 0:B], tmp[:, 0:B], 0.0, eps, ALU.max, ALU.add))
                dve.tensor_copy(q2[:, 0:B], tmp[:, 0:B]).then_inc(s_var, 1)
                dve.wait_ge(s_root, 1)
                rsqrt(scale, q2[:, 0:B], B)
                link(dve.tensor_tensor(bias, m, scale, ALU.mult))
                link(dve.tensor_scalar(bias, bias, -1.0, None, ALU.mult))
                if bn is None:
                    return
                gamma, beta, bn_eps, a, t = bn
                link(dve.tensor_scalar(cols[:], cols[:], 1.0 / n_chan, None, ALU.mult))
                mu, q = cols[:, 0:B], cols[:, B:2 * B]
                link(dve.tensor_scalar(tmp[:, 0:B], mu, 2.0, None, ALU.mult))
                link(dve.tensor_tensor(tmp[:, 0:B], tmp[:, 0:B], m, ALU.subtract))
                link(dve.tensor_tensor(tmp[:, 0:B], tmp[:, 0:B], m, ALU.mult))
                link(dve.tensor_tensor(q2[:, B:2 * B], q, tmp[:, 0:B], ALU.subtract))
                link(dve.tensor_tensor(q2[:, B:2 * B], q2[:, B:2 * B], scale, ALU.mult))
                link(dve.tensor_tensor(q2[:, B:2 * B], q2[:, B:2 * B], scale, ALU.mult))
                link(dve.tensor_tensor(q2[:, 0:B], mu, m, ALU.subtract))
                link(dve.tensor_tensor(q2[:, 0:B], q2[:, 0:B], scale, ALU.mult))
                link(dve.tensor_reduce(one[:, 0:2], q2[:].rearrange("p (k b) -> p k b", k=2), AX.X, ALU.add))
                link(dve.tensor_scalar(one[:, 0:2], one[:, 0:2], 1.0 / B, None, ALU.mult))
                link(dve.tensor_tensor(one[:, 2:3], one[:, 0:1], one[:, 0:1], ALU.mult))
                link(dve.tensor_tensor(one[:, 3:4], one[:, 1:2], one[:, 2:3], ALU.subtract))
                dve.tensor_scalar(one[:, 3:4], one[:, 3:4], 0.0, bn_eps, ALU.max, ALU.add).then_inc(s_var, 1)
                dve.wait_ge(s_root, 2)
                rsqrt(one[:, 4:5], one[:, 3:4], 1)
                link(dve.tensor_tensor(one[:, 5:6], one[:, 4:5], gamma, ALU.mult))
                link(dve.tensor_tensor(one[:, 6:7], one[:, 5:6], one[:, 0:1], ALU.mult))
                link(dve.tensor_tensor(one[:, 7:8], one[:, 6:7], beta, ALU.subtract))
                link(dve.tensor_scalar(a, scale, one[:, 5:6], None, ALU.mult))
                link(dve.tensor_tensor(t, a, m, ALU.mult))
                link(dve.tensor_scalar(t, t, one[:, 7:8], None, ALU.add))


def build_kernel(nc, x, w_qkv, w_v, w_proj, gamma, beta, w_bin, out):
    B, H = x.shape[0], x.shape[1]
    ROWS = B * H
    NP = ROWS // 2
    IT = ROWS // 8
    IPI = H // 8
    NPIX = float(H * W * (C // 32))
    xr_v = x.rearrange("b h w c -> (b h) w c")
    out_v = out.rearrange("b h w c -> (b h) w c")
    CH = min(16, H // 4)
    NCH = H // CH
    xchunks = x.rearrange("b (k r) w c -> (b k) (r w c)", r=CH).rearrange("k (p n) -> k p n", p=P)
    x1_d = nc.dram_tensor("x1_scratch", [ROWS, W, C], F32).ap()
    v_d = nc.dram_tensor("v_scratch", [4, 2, WP, K2 * 256], F16).ap()
    a_d = nc.dram_tensor("a_scratch", [2, WP, K2 * 3 * AR], F16).ap()

    def after(eng, sem, count):
        if isinstance(count, int) and count <= 0:
            return
        eng.wait_ge(sem, count)

    def place(i, u, d):
        return (u + d) % 4, i + (u + d) // 4

    with ExitStack() as ctx:
        def sb(name, shape, dt, c=ctx):
            return c.enter_context(nc.sbuf_tensor(name, shape, dt))

        def sem(name, c=ctx):
            return c.enter_context(nc.semaphore(name))

        def psum(name, shape, dt, c):
            return c.enter_context(nc.psum_tensor(name, shape, dt))

        ident = sb("ident", [P, P], F32)
        ones = sb("ones", [P, P], F32)
        group = sb("group", [P, P], F32)
        gn_scale = sb("gn_scale", [P, B], F32)
        gn_bias = sb("gn_bias", [P, B], F32)
        acc_sum = sb("acc_sum", [P, B, 256], F32)
        acc_sq = sb("acc_sq", [P, B, 256], F32)
        wbin = sb("wbin", [P, K2, C], F16)
        wscale = sb("wscale", [P, 4, C], F32)
        gam = sb("gam", [P, 1], F32)
        bet = sb("bet", [P, 1], F32)

        with ExitStack() as l0:
            wq = [sb(f"wq_{k}", [P, LOG], F16, l0) for k in "hl"]
            wv = [sb(f"wv_{k}", [P, K2 * C], F16, l0) for k in "hl"]
            wp = sb("wp", [P, 2, C], F32, l0)
            exp_scale = sb("exp_scale", [P, 1], F32, l0)
            first_row = sb("first_row", [P, IT], F32, l0)
            last_row = sb("last_row", [P, IT], F32, l0)
            band = sb("band", [P, 2, TILES, WIN, AR], F16, l0)
            vt = sb("vt", [P, 4, 2 * TILES, 256], F16, l0)
            xn = [sb(f"xn_{k}", [P, RING, W + 2], F16, l0) for k in "hl"]
            carry = sb("carry", [P, 2, 2, 256], F32, l0)

            first_pass = l0.enter_context(ExitStack())
            xc = sb("xc", [P, 4, CH, C], F32, first_pass)
            s_x = [sem(f"b_x{k}", first_pass) for k in range(4)]

            def load_chunk(sp, b, k):
                sp.dma_start(xc[:, k % 4].rearrange("p n c -> p (n c)"),
                             xchunks[bass.ds(b * NCH + k, 1)].rearrange("a p n -> (a p) n")).then_inc(s_x[k % 4], 16)

            with ExitStack() as c:
                wq_in = sb("wq_in", [P, 3, C], F32, c)
                wv_in = sb("wv_in", [P, K2, C], F32, c)
                wp_in = sb("wp_in", [P, C], F32, c)
                wp_dup = sb("wp_dup", [P, 2, 2, 2, HD], F32, c)
                wb_in = sb("wb_in", [P, K2, C], F32, c)
                wb_ge = sb("wb_ge", [P, K2, C], F32, c)
                wb_abs = sb("wb_abs", [P, K2, C], F32, c)
                wtf = sb("wtf", [P, LOG], F32, c)
                wvf = sb("wvf", [P, K2 * C], F32, c)
                top = sb("top", [P, 2], F32, c)
                top_row = sb("top_row", [2, 1], F32, c)
                top_pow = sb("top_pow", [2, 1], U32, c)
                diag = sb("diag", [2, 2], F32, c)
                pw = sb("pw", [P, 2], F32, c)
                ipw = sb("ipw", [P, 2], F32, c)
                zero = sb("zero", [8, 2 * K2 * 3 * AR], F16, c)
                ps = [psum(f"pw{k}", [P, 512], F32, c) for k in range(7)]
                s_ld = [sem(f"a_ld{k}", c) for k in range(4)]
                s_gb = sem("a_gb", c)
                s_cst = sem("a_cst", c)
                s_cst2 = sem("a_cst2", c)
                s_zero = sem("a_zero", c)
                s_pad = sem("a_pad", c)
                s_dup = sem("a_dup", c)
                s_top = sem("a_top", c)
                s_topt = sem("a_topt", c)
                s_chain = sem("a_chain", c)
                s_diag = sem("a_diag", c)
                s_pw = sem("a_pw", c)
                s_tq = sem("a_tq", c)
                s_tv = sem("a_tv", c)
                s_tp = sem("a_tp", c)
                s_f = sem("a_f", c)
                s_hi = sem("a_hi", c)
                s_bin = sem("a_bin", c)
                s_bins = sem("a_bins", c)
                s_done = sem("a_done", c)
                with nc.Block() as block:
                    @block.sync
                    def _(sp):
                        sp.dma_start(wq_in[0:108], w_qkv.rearrange("(a p) c -> p a c", p=108)).then_inc(s_ld[0], 16)
                        sp.dma_start(wv_in[:], w_v.rearrange("q i j -> i q j")).then_inc(s_ld[1], 16)
                        sp.dma_start(wp_in[:], w_proj).then_inc(s_ld[2], 16)
                        sp.dma_start(wb_in[:], w_bin.rearrange("a b i o -> i (a b) o")).then_inc(s_ld[3], 16)
                        sp.dma_start(gam[:], gamma.rearrange("(c a) -> c a", a=1)).then_inc(s_gb, 16)
                        sp.dma_start(bet[:], beta.rearrange("(c a) -> c a", a=1)).then_inc(s_gb, 16)
                        for k in range(4):
                            load_chunk(sp, 0, k)
                        sp.wait_ge(s_zero, 1)
                        sp.dma_start(v_d.rearrange("s r n c -> (s r) n c")[:, W:WP, :],
                                     zero[:, 0:2 * K2 * 256].rearrange("p (n c) -> p n c", n=2)).then_inc(s_pad, 16)
                        sp.dma_start(a_d[:, W:WP, :], zero[0:2].rearrange("p (n c) -> p n c", n=2)).then_inc(s_pad, 16)
                        sp.wait_ge(s_pad, 32)
                        sp.wait_ge(s_gb, 32)

                    @block.gpsimd
                    def _(pool):
                        pool.memset(zero[:], 0.0).then_inc(s_zero, 1)
                        pool.memset(ident[:], 0.0).then_inc(s_cst2, 1)
                        pool.memset(ones[:], 1.0).then_inc(s_cst, 1)
                        pool.memset(group[:], 1.0).then_inc(s_cst2, 1)
                        pool.wait_ge(s_cst2, 2)
                        pool.affine_select(out=ident[:], in_=ident[:], compare_op=ALU.not_equal, fill=1.0, base=0,
                                           pattern=[[-1, P]], channel_multiplier=1).then_inc(s_cst, 1)
                        gv = group[:].rearrange("p (g e) -> p g e", e=4)
                        pool.affine_select(out=gv, in_=gv, compare_op=ALU.is_ge, fill=0.0, base=0,
                                           pattern=[[-4, 32], [0, 4]], channel_multiplier=1).then_inc(s_cst2, 1)
                        pool.wait_ge(s_cst2, 3)
                        pool.affine_select(out=gv, in_=gv, compare_op=ALU.is_ge, fill=0.0, base=3,
                                           pattern=[[4, 32], [0, 4]], channel_multiplier=-1).then_inc(s_cst, 1)
                        pool.memset(xn[0][:], 0.0).then_inc(s_cst, 1)
                        pool.memset(xn[1][:], 0.0).then_inc(s_cst, 1)
                        pool.memset(carry[:], 0.0).then_inc(s_cst, 1)
                        pool.memset(acc_sum[:], 0.0).then_inc(s_cst, 1)
                        pool.memset(acc_sq[:], 0.0).then_inc(s_cst, 1)
                        pool.memset(band[:, 0].bitcast(U32), 0).then_inc(s_cst, 1)
                        pool.wait_ge(s_cst, 9)

                    @block.vector
                    def _(dve):
                        dve.memset(top[:], 0.0).then_inc(s_chain, 1)
                        dve.memset(first_row[:], 1.0).then_inc(s_chain, 1)
                        dve.memset(last_row[:], 1.0).then_inc(s_chain, 1)
                        dve.wait_ge(s_chain, 3)
                        dve.memset(first_row[:].rearrange("p (b i) -> p b i", b=B)[:, :, 0:1], 0.0).then_inc(s_chain, 1)
                        dve.memset(last_row[:].rearrange("p (b i) -> p b i", b=B)[:, :, IPI - 1:IPI], 0.0).then_inc(s_chain, 1)
                        dve.memset(band[:, 1].bitcast(U32), 0).then_inc(s_chain, 1)
                        dve.wait_ge(s_ld[0], 16)
                        dve.tensor_reduce(top[0:108, 0:1], wq_in[0:108], AX.XY, ALU.max, apply_absolute_value=True).then_inc(s_top, 1)
                        dve.wait_ge(s_ld[1], 16)
                        dve.tensor_reduce(top[:, 1:2], wv_in[:], AX.XY, ALU.max, apply_absolute_value=True).then_inc(s_top, 1)
                        dve.wait_ge(s_topt, 1)
                        dve.tensor_reduce(top_row[:], ps[0][0:2, 0:P], AX.X, ALU.max).then_inc(s_chain, 1)
                        dve.wait_ge(s_chain, 7)
                        dve.tensor_scalar(top_row[:], top_row[:], 1e-30, None, ALU.max).then_inc(s_chain, 1)
                        dve.wait_ge(s_chain, 8)
                        dve.tensor_scalar(top_pow[:], top_row[:].bitcast(U32), 0x7F800000, None, ALU.bitwise_and).then_inc(s_chain, 1)
                        dve.wait_ge(s_chain, 9)
                        dve.wait_ge(s_cst, 2)
                        dve.tensor_scalar(diag[:], ident[0:2, 0:2], top_pow[:].bitcast(F32), None, ALU.mult).then_inc(s_diag, 1)
                        dve.wait_ge(s_pw, 1)
                        dve.tensor_copy(pw[:], ps[1][:, 0:2]).then_inc(s_chain, 1)
                        dve.wait_ge(s_chain, 10)
                        dve.reciprocal(ipw[:], pw[:]).then_inc(s_chain, 1)
                        dve.tensor_scalar(exp_scale[:], pw[:, 0:1], float(HD) ** -0.5, None, ALU.mult).then_inc(s_chain, 1)
                        dve.wait_ge(s_chain, 12)
                        dve.wait_ge(s_tq, 1)
                        lv = ps[2][:, 0:LOG].rearrange("p (h i j q) -> p q j i h", h=HEADS, i=3, j=3)
                        for q in range(K2):
                            dve.tensor_scalar(wtf[:, q * NPH:(q + 1) * NPH].rearrange("p (j i h) -> p j i h", j=3, i=3),
                                              lv[:, q], ipw[:, 0:1], None, ALU.mult).then_inc(s_f, 1)
                        dve.wait_ge(s_tv, 1)
                        for g in range(3):
                            dve.tensor_scalar(wvf[:, g * 384:(g + 1) * 384], ps[3 + g][:, 0:384], ipw[:, 1:2], None,
                                              ALU.mult).then_inc(s_f, 1)
                        dve.wait_ge(s_tp, 1)
                        dve.tensor_scalar(wp[:].rearrange("p a o -> p (a o)"), ps[6][:, 0:256], pw[:, 1:2], None, ALU.mult).then_inc(s_done, 1)
                        dve.wait_ge(s_hi, 2)
                        dve.tensor_tensor(wq[1][:], wtf[:], wq[0][:], ALU.subtract).then_inc(s_done, 1)
                        dve.tensor_tensor(wv[1][:], wvf[:], wv[0][:], ALU.subtract).then_inc(s_done, 1)
                        dve.wait_ge(s_ld[3], 16)
                        dve.tensor_scalar(wb_ge[:], wb_in[:], 0.0, 2.0, ALU.is_ge, ALU.mult).then_inc(s_chain, 1)
                        dve.wait_ge(s_chain, 13)
                        dve.tensor_scalar(wbin[:], wb_ge[:], -1.0, None, ALU.add).then_inc(s_done, 1)
                        dve.wait_ge(s_bins, 1)
                        for r in range(4):
                            dve.tensor_scalar(wscale[:, r, :], ps[0][:, 256:384], 1.0 / (K2 * C), None, ALU.mult).then_inc(s_done, 1)
                        dve.wait_ge(s_done, 8)

                    @block.scalar
                    def _(act):
                        act.wait_ge(s_ld[2], 16)
                        for hl in range(2):
                            act.activation(wp_dup[:, :, :, hl, :].rearrange("o a h d -> o (a h) d"),
                                           wp_in[:].rearrange("o (h d) -> o h d", d=HD), ACT.Copy).then_inc(s_dup, 1)
                        act.wait_ge(s_ld[3], 16)
                        act.activation(wb_abs[:], wb_in[:], ACT.Abs).then_inc(s_bin, 1)
                        act.wait_ge(s_f, K2 + 3)
                        act.activation(wq[0][:], wtf[:], ACT.Copy).then_inc(s_hi, 1)
                        act.activation(wv[0][:], wvf[:], ACT.Copy).then_inc(s_hi, 1)

                    @block.tensor
                    def _(pe):
                        pe.wait_ge(s_cst, 2)
                        pe.wait_ge(s_top, 2)
                        pe.transpose(ps[0][0:2, 0:P], top[:], ident[:]).then_inc(s_topt, 1)
                        for a in range(3):
                            last = pe.transpose(ps[2][:, a * 108:(a + 1) * 108], wq_in[0:108, a, :], ident[0:108, 0:108])
                        last.then_inc(s_tq, 1)
                        for q in range(K2):
                            last = pe.transpose(ps[3 + q // 3][:, (q % 3) * C:(q % 3 + 1) * C], wv_in[:, q, :], ident[:])
                        last.then_inc(s_tv, 1)
                        pe.wait_ge(s_dup, 2)
                        for a in range(2):
                            last = pe.transpose(ps[6][:, a * C:(a + 1) * C],
                                                wp_dup[:, a].rearrange("o h l d -> o (h l d)"), ident[:])
                        last.then_inc(s_tp, 1)
                        pe.wait_ge(s_diag, 1)
                        pe.matmul(ps[1][:, 0:2], ones[0:2, :], diag[:], start=True, stop=True).then_inc(s_pw, 1)
                        pe.wait_ge(s_bin, 1)
                        for q in range(K2):
                            last = pe.matmul(ps[0][:, 256:384], ones[:], wb_abs[:, q, :], start=q == 0, stop=q == K2 - 1)
                        last.then_inc(s_bins, 1)

            with ExitStack() as c:
                xsq = sb("xsq", [P, 2, CH, C], F32, c)
                part = sb("part", [P, NCH, C], F32, c)
                sums = sb("sums", [P, B, C], F32, c)
                sqs = sb("sqs", [P, B, C], F32, c)
                ps_sum = psum("ps_sum", [P, 512], F32, c)
                s_sum = sem("b_sum", c)
                s_sq = sem("b_sq", c)
                s_part = sem("b_part", c)
                s_img = sem("b_img", c)
                s_isq = sem("b_isq", c)
                with nc.Block() as block:
                    @block.sync
                    def _(sp):
                        def image(b, first=0):
                            for k in range(NCH):
                                after(sp, s_sum, NCH * b + k - 3)
                                after(sp, s_sq, NCH * b + k - 3)
                                if k >= first:
                                    load_chunk(sp, b, k)

                        image(0, 4)
                        with sp.Fori(1, B) as b:
                            image(b)

                    @block.tensor
                    def _(pe):
                        def image(b):
                            for k in range(NCH):
                                pe.wait_ge(s_x[k % 4], 16 * ((b * NCH + k) // 4 + 1))
                                if k == 0:
                                    after(pe, s_img, b)
                                for g in range(CH // 4):
                                    last = pe.matmul(ps_sum[:], ones[:], xc[:, k % 4, 4 * g:4 * g + 4, :].rearrange("p r c -> p (r c)"),
                                                     start=k == 0 and g == 0, stop=k == NCH - 1 and g == CH // 4 - 1)
                                last.then_inc(s_sum, 1)

                        image(0)
                        with pe.Fori(1, B) as b:
                            image(b)

                    @block.scalar
                    def _(act):
                        def image(b):
                            for k in range(NCH):
                                act.wait_ge(s_x[k % 4], 16 * ((b * NCH + k) // 4 + 1))
                                after(act, s_part, NCH * b + k - 1)
                                act.activation(xsq[:, k % 2], xc[:, k % 4], ACT.Square).then_inc(s_sq, 1)

                        image(0)
                        with act.Fori(1, B) as b:
                            image(b)

                    @block.vector
                    def _(dve):
                        def image(b):
                            after(dve, s_isq, b)
                            for k in range(NCH):
                                dve.wait_ge(s_sq, NCH * b + k + 1)
                                dve.tensor_reduce(part[:, k, :], xsq[:, k % 2].rearrange("p r c -> p c r"), AX.X, ALU.add).then_inc(s_part, 1)
                            dve.wait_ge(s_sum, NCH * (b + 1))
                            dve.tensor_reduce(sums[:, bass.ds(b, 1), :].rearrange("p a c -> p (a c)"), ps_sum[:].rearrange("p (r c) -> p c r", c=C), AX.X, ALU.add).then_inc(s_img, 1)
                            dve.wait_ge(s_part, NCH * (b + 1))
                            dve.tensor_reduce(sqs[:, bass.ds(b, 1), :].rearrange("p a c -> p (a c)"), part[:].rearrange("p k c -> p c k"), AX.X, ALU.add).then_inc(s_isq, 1)

                        image(0)
                        with dve.Fori(1, B) as b:
                            image(b)

                norm_params(nc, "c", B, NPIX, 1.0, EPS_GN, [sums[0:1]], [sqs[:]], ones, group,
                            gn_scale[:], gn_bias[:])

            first_pass.close()

            with ExitStack() as c:
                x_in = sb("x_in", [P, 4, 2, C], F32, c)
                x_keep = sb("x_keep", [P, XR, 4, 2, C], F32, c)
                x1_s = sb("x1_s", [P, 4, 2, C], F32, c)
                x1_sq = sb("x1_sq", [P, 256], F32, c)
                xf = sb("xf", [P, 2, 2, W], F32, c)
                v_s = sb("v_s", [P, 2, 2, K2 * 256], F16, c)
                a_s = sb("a_s", [P, 2, K2 * 3, 4, DH, 2], F16, c)
                e = sb("e", [P, 2, 2, LOG], F32, c)
                an = sb("an", [P, 2, 2, LOG], F32, c)
                gn_now = sb("gn_now", [P, 2], F32, c)
                mx = sb("mx", [P, 2, NPH], F32, c)
                sm = sb("sm", [P, 2, NPH], F32, c)
                ri = sb("ri", [P, 2, 2, NPH], F32, c)
                y_s = sb("y_s", [P, 2, 2, 256], F32, c)
                ps_y = [psum(f"ps_y{k}", [P, 2, 512], F32, c) for k in range(2)]
                ps_v = [psum(f"ps_v{k}", [P, 512], F32, c) for k in range(2)]
                ps_l = psum("ps_l", [P, 512], F32, c)
                ps_m = psum("ps_m", [P, 512], F32, c)
                s_xl = [sem(f"x_loaded{k}", c) for k in range(4)]
                s_wv = [[sem(f"v_written{k}_row{r}", c) for r in range(2)] for k in range(4)]
                s_wa = [sem(f"a_written{k}", c) for k in range(2)]
                s_rv = [sem(f"vt_loaded{k}", c) for k in range(4)]
                s_ra = [sem(f"band_loaded{k}", c) for k in range(2)]
                s_st = [sem(f"x1_stored{k}", c) for k in range(4)]
                t_done = sem("t_done", c)
                v_done = sem("v_done", c)
                l_done = sem("l_done", c)
                y_done = sem("y_done", c)
                z_done = sem("z_done", c)
                e_done = sem("e_done", c)
                xhi_done = sem("xhi_done", c)
                keep_done = sem("keep_done", c)
                vhi_done = sem("vhi_done", c)
                carry_done = sem("carry_done", c)
                ahi_done = sem("ahi_done", c)
                g_done = sem("g_done", c)
                xf_done = sem("xf_done", c)
                vlo_done = sem("vlo_done", c)
                mx_done = sem("mx_done", c)
                d_done = sem("d_done", c)
                sm_done = sem("sm_done", c)
                r_raw = sem("r_raw", c)
                r_done = sem("r_done", c)
                fold_done = sem("fold_done", c)
                x1_done = sem("x1_done", c)
                an_done = sem("an_done", c)
                xlo_done = sem("xlo_done", c)
                alo_done = sem("alo_done", c)
                sq_done = sem("sq_done", c)
                stat_done = sem("stat_done", c)

                FRONT, BACK = (-1, 0, 1, 2), (IT - 1, IT, IT + 1)

                def valid(i, u, d):
                    return not isinstance(i, int) or 0 <= 4 * i + u + d < NP

                def run_steps(eng, step):
                    for i in FRONT:
                        for u in range(4):
                            step(i, u)
                    if IT - 1 > 3:
                        with eng.Fori(3, IT - 1) as i:
                            for u in range(4):
                                step(i, u)
                    for i in BACK:
                        for u in range(4):
                            step(i, u)

                def a_rows(slot, l):
                    return a_s[:, slot // 2, :, 2 * (slot % 2):2 * (slot % 2) + 2, :, l].rearrange("p k r c -> p r k c")

                def least(i, count):
                    return min(count, NP) if isinstance(i, int) else count

                with nc.Block() as block:
                    @block.sync
                    def _(sp):
                        def load_x(i, u, d):
                            slot, it = place(i, u, d)
                            p = 4 * i + u + d
                            if isinstance(i, int):
                                after(sp, keep_done, p - 3)
                            sp.dma_start(x_in[:, slot], xr_v[bass.ds(2 * p, 2)].rearrange("r w c -> w r c")).then_inc(s_xl[slot], 16)

                        def step(i, u):
                            s = 4 * i + u
                            after(sp, y_done, least(i, s - 5))
                            if valid(i, u, 4):
                                load_x(i, u, 4)
                            if valid(i, u, -2):
                                slot, it = place(i, u, -2)
                                for r in range(2):
                                    sp.wait_ge(s_wv[slot][r], 16 * (it + 1))
                                sp.dma_start(vt[0:KT, slot], v_d[slot].rearrange("r n c -> (r n c)").rearrange("(t k c) -> k t c", k=KT, c=256)).then_inc(s_rv[slot], 16)
                            if valid(i, u, -2) and u % 2 == 1:
                                two = slot // 2
                                sp.wait_ge(s_wa[two], 16 * (it + 1))
                                av = a_d[two].rearrange("(t j) (q c) -> j q t c", j=JT, q=K2)
                                for j in range(JT):
                                    sp.dma_start(band[K2 * j:K2 * (j + 1), two, :, j:j + 3, :].rearrange("q t m c -> q t (m c)"),
                                                 av[j]).then_inc(s_ra[two], 16)
                            if valid(i, u, -1) and u % 2 == 0:
                                slot, it = place(i, u, -1)
                                two = slot // 2
                                sp.wait_ge(alo_done, s)
                                sp.dma_start(a_d[two][0:W], a_s[:, two].rearrange("p k r d l -> p (k r d l)")).then_inc(s_wa[two], 16)
                            if valid(i, u, -7):
                                slot, it = place(i, u, -7)
                                sp.wait_ge(x1_done, s - 6)
                                sp.dma_start(x1_d[bass.ds(2 * s - 14, 2)].rearrange("r w c -> w r c"), x1_s[:, slot]).then_inc(s_st[slot], 16)

                        run_steps(sp, step)
                        for k in range(4):
                            sp.wait_ge(s_st[k], 16 * IT)

                    @block.tensor
                    def _(pe):
                        def transposes(i, u):
                            slot, it = place(i, u, 2)
                            s = 4 * i + u
                            pe.wait_ge(s_xl[slot], 16 * (it + 1))
                            after(pe, xf_done, s + 2)
                            after(pe, x1_done, s - 7)
                            for r in range(2):
                                last = pe.transpose(ps_m[:, 256 + r * W:256 + (r + 1) * W], x_in[:, slot, r, :], ident[:])
                            last.then_inc(t_done, 1)

                        def values(i, u, g):
                            s = 4 * i + u
                            r, di = g // 3, g % 3
                            after(pe, vlo_done, 6 * s + g - 1)
                            if g % 3 == 0:
                                pe.wait_ge(xlo_done, least(i, s + 1 + r))
                            row = (2 * u + r + di - 1) % RING
                            for dj in range(3):
                                q = 3 * di + dj
                                for n, (a, b) in enumerate(((0, 0), (0, 1), (1, 0))):
                                    last = pe.matmul(ps_v[g % 2][:, dj * C:(dj + 1) * C], xn[a][:, row, dj:dj + W],
                                                     wv[b][:, q * C:(q + 1) * C], start=n == 0, stop=n == 2)
                            last.then_inc(v_done, 1)

                        def logits(i, u, r):
                            s = 4 * i + u
                            after(pe, d_done, 2 * s + r)
                            row = (2 * u + r) % RING
                            for n, (a, b) in enumerate(((0, 0), (0, 1), (1, 0))):
                                last = pe.matmul(ps_l[:, 0:LOG], xn[a][:, row, 1:1 + W], wq[b][:], start=n == 0, stop=n == 2)
                            last.then_inc(l_done, 1)

                        CUTS = (0, 3, 6, 8, 10, 13, 16, 18, 2 * TILES)

                        def bands(i, u, part):
                            slot, it = place(i, u, -5)
                            s = 4 * i + u
                            y = ps_y[(u - 5) % 2]
                            if part == 0:
                                pe.wait_ge(s_rv[slot], 16 * (it + 1))
                                pe.wait_ge(s_ra[slot // 2], 16 * JT * (it + 1))
                                after(pe, carry_done, s - 6)
                            for tile in range(CUTS[part], CUTS[part + 1]):
                                r, t = tile // TILES, tile % TILES
                                lo = 1 if t == 0 else 0
                                hi = min(WIN, W + 1 - JT * t)
                                col = JT * t - 1 + lo
                                row = (slot % 2) * 2 + r
                                win = band[0:KT, slot // 2, t, :, row * 2 * DH:(row + 1) * 2 * DH].rearrange(
                                    "k m (i h l) -> k h l i m", i=3, h=HEADS, l=2)
                                for h in range(HEADS):
                                    for l in range(2):
                                        o = y[64 * (h % 2):64 * (h % 2) + 64, h // 2, :].rearrange("p (s m) -> p s m", m=W)
                                        last = pe.matmul(o[:, r:r + 3, col:col + hi - lo],
                                                         vt[0:KT, slot, tile, 64 * h:64 * h + 64],
                                                         win[:, h, l, :, lo:hi], start=tile == 0 and l == 0,
                                                         stop=tile == 2 * TILES - 1 and l == 1, skip_group_check=True)
                            if part == 7:
                                last.then_inc(y_done, 1)

                        def project(i, u):
                            s = 4 * i + u
                            pe.wait_ge(fold_done, s - 5)
                            pe.wait_ge(xf_done, least(i, s + 3))
                            after(pe, x1_done, s - 7)
                            q0, q1 = (u + 1) % 2, u % 2
                            for r, (slot, off) in enumerate(((q0, W), (q1, 0))):
                                for a in range(2):
                                    last = pe.matmul(ps_m[:, r * C:(r + 1) * C], y_s[:, slot, a, off:off + W], wp[:, a, :],
                                                     start=a == 0, stop=a == 1)
                            last.then_inc(z_done, 1)

                        def step(i, u):
                            if valid(i, u, 2):
                                transposes(i, u)
                            for n in range(8):
                                if valid(i, u, 0):
                                    if n % 4 < 3:
                                        values(i, u, 3 * (n // 4) + n % 4)
                                    else:
                                        logits(i, u, n // 4)
                                if n == 4 and valid(i, u, -7):
                                    project(i, u)
                                if valid(i, u, -5):
                                    bands(i, u, n)

                        run_steps(pe, step)

                    @block.scalar
                    def _(act):
                        def step(i, u):
                            s = 4 * i + u
                            if valid(i, u, 2):
                                slot, it = place(i, u, 2)
                                act.wait_ge(g_done, 2 * it + 2)
                                after(act, v_done, 6 * s)
                                act.wait_ge(t_done, s + 3)
                                act.activation(xn[0][:, 2 * slot:2 * slot + 2, 1:1 + W], ps_m[:, 256:512].rearrange("p (r w) -> p r w", r=2),
                                               ACT.Identity, bias=gn_now[:, 1:2], scale=gn_now[:, 0:1]).then_inc(xhi_done, 1)
                            for g in range(6):
                                if g == 3 and valid(i, u, 2):
                                    slot, it = place(i, u, 2)
                                    act.activation(x_keep[:, bass.ds(it % XR, 1), slot].rearrange("p a r c -> p (a r c)"),
                                                   x_in[:, slot].rearrange("p r c -> p (r c)"), ACT.Copy).then_inc(keep_done, 1)
                                if g == 1 and valid(i, u, -1):
                                    act.wait_ge(d_done, 2 * s)
                                    ep = e[:, (u - 1) % 2].rearrange("p r k -> p (r k)")
                                    act.activation(ep, ep, ACT.Exp, scale=exp_scale[:, 0:1]).then_inc(e_done, 1)
                                if g == 1 and valid(i, u, -1):
                                    slot, it = place(i, u, -1)
                                    act.wait_ge(vlo_done, 6 * s)
                                    act.dma_start(v_d[slot, 1, 0:W], v_s[:, (u - 1) % 2, 1]).then_inc(s_wv[slot][1], 16)
                                if g == 4 and valid(i, u, 0):
                                    slot, it = place(i, u, 0)
                                    act.wait_ge(vlo_done, 6 * s + 3)
                                    after(act, s_rv[slot], 16 * it)
                                    act.dma_start(v_d[slot, 0, 0:W], v_s[:, u % 2, 0]).then_inc(s_wv[slot][0], 16)
                                if g == 2 and valid(i, u, -6):
                                    act.wait_ge(fold_done, s - 5)
                                    act.activation(carry[:, u % 2], ps_y[u % 2][:, :, 256:512], ACT.Copy).then_inc(carry_done, 1)
                                if g == 5 and valid(i, u, -1):
                                    slot, it = place(i, u, -1)
                                    act.wait_ge(an_done, s)
                                    after(act, s_wa[slot // 2], 16 * it)
                                    act.activation(a_rows(slot, 0), an[:, (u - 1) % 2].rearrange("p r (k c) -> p r k c", c=DH),
                                                   ACT.Copy).then_inc(ahi_done, 1)
                                if valid(i, u, 0):
                                    slot, it = place(i, u, -2)
                                    act.wait_ge(v_done, 6 * s + g + 1)
                                    if g % 3 == 0 and valid(i, u, -2):
                                        act.wait_ge(s_wv[slot][g // 3], 16 * (it + 1))
                                    vp = v_s[:, u % 2, g // 3, 768 * (g % 3):768 * (g % 3 + 1)].rearrange("p (h l d) -> p h l d", l=2, d=HD)
                                    act.activation(vp[:, :, 0, :], ps_v[g % 2][:, 0:384].rearrange("p (h d) -> p h d", d=HD),
                                                   ACT.Copy).then_inc(vhi_done, 1)

                        run_steps(act, step)

                    @block.vector
                    def _(dve):
                        def softmax_top(i, u, r):
                            s = 4 * i + u
                            dve.wait_ge(l_done, 2 * s + r + 1)
                            after(dve, d_done, 2 * s + r - 1)
                            if r == 0:
                                after(dve, an_done, s - 1)
                            lv = ps_l[:, 0:LOG].rearrange("p (q k) -> p q k", q=K2)
                            dve.tensor_reduce(mx[:, r, :], lv.rearrange("p q k -> p k q"), AX.X, ALU.max).then_inc(mx_done, 1)
                            dve.wait_ge(mx_done, 2 * s + r + 1)
                            dve.tensor_tensor(e[:, u % 2, r, :].rearrange("p (q k) -> p q k", q=K2), lv,
                                              mx[:, r, :].unsqueeze(1).to_broadcast([P, K2, NPH]), ALU.subtract).then_inc(d_done, 1)

                        def softmax_sum(i, u):
                            s = 4 * i + u
                            v = (u - 1) % 2
                            dve.wait_ge(e_done, s)
                            after(dve, an_done, s - 2)
                            dve.tensor_reduce(sm[:], e[:, v].rearrange("p r (q k) -> p r k q", q=K2), AX.X, ALU.add).then_inc(sm_done, 1)
                            dve.wait_ge(sm_done, s)
                            edge = u in (0, 1)
                            dve.reciprocal(ri[:, v], sm[:]).then_inc(r_raw if edge else r_done, 1)
                            if edge:
                                it = i if u == 1 else i - 1
                                row, di, keep = (0, 0, first_row) if u == 1 else (1, 2, last_row)
                                ev = e[:, v, row, 3 * di * NPH:3 * (di + 1) * NPH]
                                dve.tensor_scalar(ev, ev, keep[:, bass.ds(it, 1)], None, ALU.mult).then_inc(r_raw, 1)
                                dve.wait_ge(r_raw, 4 * it + (2 if u == 1 else 4))
                                rv = ri[:, v, row, :].rearrange("p (j i h) -> p j i h", j=3, i=3)[:, :, di, :]
                                dve.tensor_scalar(rv, rv, keep[:, bass.ds(it, 1)], None, ALU.mult).then_inc(r_done, 1)

                        def step(i, u):
                            s = 4 * i + u
                            if valid(i, u, 2):
                                slot, it = place(i, u, 2)
                                if u == 2:
                                    img = it // IPI
                                    for k, par in enumerate((gn_scale, gn_bias)):
                                        dve.tensor_scalar(gn_now[:, k:k + 1], par[:, bass.ds(img, 1)], 1.0, None, ALU.mult).then_inc(g_done, 1)
                                    dve.wait_ge(g_done, 2 * it + 2)
                                dve.wait_ge(xhi_done, s + 3)
                                after(dve, xlo_done, s + 1)
                                dve.tensor_scalar(xf[:, u % 2].rearrange("p r w -> p (r w)"), ps_m[:, 256:512],
                                                  gn_now[:, 0:1], gn_now[:, 1:2], ALU.mult, ALU.add).then_inc(xf_done, 1)
                            for g in range(6):
                                if g == 1 and valid(i, u, -6):
                                    dve.wait_ge(y_done, s - 5)
                                    after(dve, carry_done, s - 6)
                                    after(dve, z_done, s - 7)
                                    dve.tensor_tensor(y_s[:, u % 2], ps_y[u % 2][:, :, 0:256], carry[:, (u - 1) % 2],
                                                      ALU.add).then_inc(fold_done, 1)
                                elif g == 1 and isinstance(i, int) and s - 6 == NP:
                                    dve.wait_ge(carry_done, NP)
                                    dve.wait_ge(z_done, NP - 1)
                                    dve.tensor_copy(y_s[:, NP % 2, :, 0:W], carry[:, (NP - 1) % 2, :, 0:W]).then_inc(fold_done, 1)
                                if g == 2 and valid(i, u, -1):
                                    softmax_sum(i, u)
                                if g == 3 and valid(i, u, 0):
                                    softmax_top(i, u, 0)
                                if g == 4 and valid(i, u, -7):
                                    slot, it = place(i, u, -7)
                                    dve.wait_ge(z_done, s - 6)
                                    dve.wait_ge(keep_done, s - 6)
                                    after(dve, s_st[slot], 16 * it)
                                    after(dve, stat_done, s - 10)
                                    dve.tensor_tensor(x1_s[:, slot].rearrange("p r c -> p (r c)"), ps_m[:, 0:256],
                                                      x_keep[:, bass.ds(it % XR, 1), slot].rearrange("p a r c -> p (a r c)"), ALU.add).then_inc(x1_done, 1)
                                if valid(i, u, 0):
                                    dve.wait_ge(vhi_done, 6 * s + g + 1)
                                    vp = v_s[:, u % 2, g // 3, 768 * (g % 3):768 * (g % 3 + 1)].rearrange("p (h l d) -> p h l d", l=2, d=HD)
                                    dve.tensor_tensor(vp[:, :, 1, :], ps_v[g % 2][:, 0:384].rearrange("p (h d) -> p h d", d=HD),
                                                      vp[:, :, 0, :], ALU.subtract).then_inc(vlo_done, 1)
                            if valid(i, u, 0):
                                softmax_top(i, u, 1)

                        run_steps(dve, step)

                    @block.gpsimd
                    def _(pool):
                        def step(i, u):
                            s = 4 * i + u
                            v = (u - 1) % 2
                            if valid(i, u, -1):
                                pool.wait_ge(r_done, s)
                                after(pool, ahi_done, s - 2)
                                after(pool, alo_done, s - 2)
                                pool.tensor_tensor(an[:, v].rearrange("p r (q k) -> p r q k", q=K2),
                                                   e[:, v].rearrange("p r (q k) -> p r q k", q=K2),
                                                   ri[:, v].unsqueeze(2).to_broadcast([P, 2, K2, NPH]),
                                                   ALU.mult).then_inc(an_done, 1)
                            if valid(i, u, 2):
                                slot, it = place(i, u, 2)
                                pool.wait_ge(xf_done, s + 3)
                                after(pool, v_done, 6 * s)
                                pool.tensor_tensor(xn[1][:, 2 * slot:2 * slot + 2, 1:1 + W], xf[:, u % 2],
                                                   xn[0][:, 2 * slot:2 * slot + 2, 1:1 + W], ALU.subtract).then_inc(xlo_done, 1)
                            if valid(i, u, -7):
                                slot, it = place(i, u, -7)
                                img = it // IPI
                                pool.wait_ge(x1_done, s - 6)
                                after(pool, stat_done, s - 7)
                                x1p = x1_s[:, slot].rearrange("p r c -> p (r c)")
                                sum_p, sq_p = (t[:, bass.ds(img, 1), :].rearrange("p a c -> p (a c)") for t in (acc_sum, acc_sq))
                                pool.tensor_tensor(x1_sq[:], x1p, x1p, ALU.mult).then_inc(sq_done, 1)
                                pool.tensor_tensor(sum_p, sum_p, x1p, ALU.add).then_inc(sq_done, 1)
                                pool.wait_ge(sq_done, 2 * (s - 6))
                            if valid(i, u, -1):
                                pool.wait_ge(ahi_done, s)
                                slot, it = place(i, u, -1)
                                pool.tensor_tensor(a_rows(slot, 1), an[:, v].rearrange("p r (k c) -> p r k c", c=DH),
                                                   a_rows(slot, 0), ALU.subtract).then_inc(alo_done, 1)
                            if valid(i, u, -7):
                                pool.tensor_tensor(sq_p, sq_p, x1_sq[:], ALU.add).then_inc(stat_done, 1)

                        run_steps(pool, step)

        bin_a = sb("bin_a", [P, B], F32)
        bin_t = sb("bin_t", [P, B], F32)
        norm_params(nc, "d", B, NPIX, float(H * W), EPS_GN, [acc_sum[:, :, 0:C], acc_sum[:, :, C:2 * C]],
                    [acc_sq[:, :, 0:C], acc_sq[:, :, C:2 * C]], ones, group, gn_scale[:], gn_bias[:],
                    (gam[:], bet[:], EPS_BN, bin_a[:], bin_t[:]))

        NG = ROWS // 4
        GPI = 8
        ITG = NG // GPI
        PER = H // (4 * GPI)
        RR = 4 * GPI
        with ExitStack() as c:
            ident16 = sb("ident16", [P, P], F16, c)
            diag_at = sb("diag_at", [P, 2, B, C], F32, c)
            rows_at = sb("rows_at", [P, B, 2, C], F32, c)
            now_at = sb("now_at", [P, 2, C], F32, c)
            first = sb("first", [P, ITG], F32, c)
            final = sb("final", [P, ITG], F32, c)
            x1 = sb("x1", [P, GPI, 4, C], F32, c)
            ax = sb("ax", [P, 2, 4, C], F32, c)
            sg = sb("sg", [P, 2, 4, C], F16, c)
            xb = sb("xb", [P, RR, W + 2], F16, c)
            above = sb("above", [P, W + 2], F16, c)
            below = sb("below", [P, W + 2], F16, c)
            conv = sb("conv", [P, 2, 4 * C], F32, c)
            o_s = sb("o_s", [P, 4, 4, C], F32, c)
            ps_at = [psum(f"ps_at{k}", [P, 512], F32, c) for k in range(2)]
            ps_t = [psum(f"ps_t{k}", [P, 512], F32, c) for k in range(2)]
            ps_c = [psum(f"ps_c{k}", [P, 512], F32, c) for k in range(2)]
            s_init = sem("init", c)
            s_dg = sem("diag_done", c)
            s_rows = sem("rows_summed", c)
            s_now = sem("now_done", c)
            s_x1 = [sem(f"x1_in{k}", c) for k in range(GPI)]
            s_out = [sem(f"out_stored{k}", c) for k in range(4)]
            ax_done = sem("ax_done", c)
            sg_done = sem("sg_done", c)
            tt_done = sem("tt_done", c)
            b_done = sem("b_done", c)
            h_done = sem("h_done", c)
            c_done = sem("c_done", c)
            m_done = sem("m_done", c)
            o_done = sem("o_done", c)

            def run_groups(eng, step):
                for i in (-1, 0):
                    for u in range(GPI):
                        step(i, u)
                if ITG > 2:
                    with eng.Fori(1, ITG - 1) as i:
                        for u in range(GPI):
                            step(i, u)
                for i in (ITG - 1, ITG):
                    for u in range(GPI):
                        step(i, u)

            def there(i, u, d):
                return not isinstance(i, int) or 0 <= GPI * i + u + d < NG

            def home(i, u, d):
                return (u + d) % GPI, i + (u + d) // GPI

            with nc.Block() as block:
                @block.sync
                def _(sp):
                    def step(i, u):
                        g = GPI * i + u
                        if there(i, u, 6):
                            slot, it = home(i, u, 6)
                            after(sp, o_done, g - 1)
                            sp.dma_start(x1[:, slot], x1_d[bass.ds(4 * g + 24, 4)].rearrange("r w c -> w r c")).then_inc(s_x1[slot], 16)
                        if there(i, u, -1):
                            sp.wait_ge(o_done, g)
                            sp.dma_start(out_v[bass.ds(4 * g - 4, 4)].rearrange("r w c -> w r c"), o_s[:, (u - 1) % 4]).then_inc(s_out[(u - 1) % 4], 16)

                    run_groups(sp, step)
                    for k in range(4):
                        sp.wait_ge(s_out[k], 16 * (NG // 4))

                @block.tensor
                def _(pe):
                    for k in range(2):
                        pe.wait_ge(s_dg, B * (k + 1))
                        pe.matmul(ps_at[k][:, 0:B * C], ones[:], diag_at[:, k].rearrange("p b c -> p (b c)"),
                                  start=True, stop=True).then_inc(s_rows, 1)
                    pe.wait_ge(s_init, 6)

                    def step(i, u):
                        g = GPI * i + u
                        if there(i, u, 2):
                            pe.wait_ge(sg_done, g + 3)
                            after(pe, b_done, g + 1)
                            for r in range(4):
                                last = pe.matmul(ps_t[u % 2][:, r * W:(r + 1) * W], sg[:, u % 2, r, :], ident16[:],
                                                 start=True, stop=True)
                            last.then_inc(tt_done, 1)
                        if there(i, u, 0):
                            pe.wait_ge(b_done, min(g + 2, NG) if isinstance(i, int) else g + 2)
                            after(pe, m_done, g - 1)
                            if u == 0:
                                pe.wait_ge(h_done, 2 * i + 1)
                            if u == GPI - 1:
                                pe.wait_ge(h_done, 2 * i + 2)
                            for r in range(4):
                                row = 4 * u + r
                                o = ps_c[u % 2][:, r * C:(r + 1) * C]
                                for di in range(3):
                                    src = above[:] if row + di == 0 else below[:] if row + di == RR + 1 else xb[:, row + di - 1, :]
                                    for dj in range(3):
                                        last = pe.matmul(o, src[:, dj:dj + W], wbin[:, 3 * di + dj, :],
                                                         start=di == 0 and dj == 0, stop=di == 2 and dj == 2)
                            last.then_inc(c_done, 1)

                    run_groups(pe, step)

                @block.scalar
                def _(act):
                    act.wait_ge(s_init, 6)

                    def step(i, u):
                        g = GPI * i + u
                        if there(i, u, 2):
                            slot, it = home(i, u, 2)
                            after(act, c_done, g - 4)
                            if slot in (GPI - 1, 0):
                                after(act, h_done, 2 * i + 1)
                            act.wait_ge(tt_done, g + 3)
                            act.activation(xb[:, 4 * slot:4 * slot + 4, 1:1 + W], ps_t[u % 2][:].rearrange("p (r w) -> p r w", r=4),
                                           ACT.Copy, bias=-1.0, scale=2.0).then_inc(b_done, 1)

                    run_groups(act, step)

                @block.vector
                def _(dve):
                    for k, par in enumerate((bin_a, bin_t)):
                        for b in range(B):
                            dve.tensor_scalar(diag_at[:, k, b, :], ident[:], par[:, b:b + 1], None, ALU.mult).then_inc(s_dg, 1)
                    dve.memset(first[:], -1.0).then_inc(s_init, 1)
                    dve.memset(final[:], -1.0).then_inc(s_init, 1)
                    dve.memset(xb[:], 1.0).then_inc(s_init, 1)
                    dve.tensor_copy(ident16[:], ident[:]).then_inc(s_init, 1)
                    dve.wait_ge(s_init, 2)
                    dve.memset(first[:].rearrange("p (b i) -> p b i", b=B)[:, :, 0:1], 1.0).then_inc(s_init, 1)
                    dve.memset(final[:].rearrange("p (b i) -> p b i", b=B)[:, :, PER - 1:PER], 1.0).then_inc(s_init, 1)
                    for k in range(2):
                        dve.wait_ge(s_rows, k + 1)
                        dve.tensor_copy(rows_at[:, :, k, :], ps_at[k][:, 0:B * C].rearrange("p (b c) -> p b c", b=B)).then_inc(s_init, 1)
                    dve.wait_ge(s_init, 8)

                    def step(i, u):
                        g = GPI * i + u
                        if there(i, u, 3):
                            slot, it = home(i, u, 3)
                            if slot == 0:
                                img = it // PER
                                after(dve, sg_done, g + 3)
                                dve.tensor_scalar(now_at[:].rearrange("p k c -> p (k c)"),
                                                  rows_at[:, bass.ds(img, 1)].rearrange("p b k c -> p (b k c)"),
                                                  1.0, None, ALU.mult).then_inc(s_now, 1)
                                dve.wait_ge(s_now, it + 1)
                            dve.wait_ge(s_x1[slot], 16 * (it + 1))
                            v = (u + 3) % 2
                            after(dve, sg_done, g + 2)
                            dve.tensor_tensor(ax[:, v], x1[:, slot], now_at[:, 0, :].unsqueeze(1).to_broadcast([P, 4, C]),
                                              ALU.mult).then_inc(ax_done, 1)
                            dve.wait_ge(ax_done, g + 4)
                            after(dve, tt_done, g + 2)
                            dve.tensor_tensor(sg[:, v], ax[:, v], now_at[:, 1, :].unsqueeze(1).to_broadcast([P, 4, C]),
                                              ALU.is_ge).then_inc(sg_done, 1)
                        if u == GPI - 1 and there(i, u, 1):
                            after(dve, c_done, g - GPI + 2)
                            after(dve, b_done, g + 1)
                            dve.tensor_scalar(above[:], xb[:, RR - 1, :], first[:, bass.ds(i + 1, 1)], None, ALU.max).then_inc(h_done, 1)
                        if u == GPI - 2 and there(i, u, 0):
                            after(dve, c_done, g - GPI + 2)
                            dve.wait_ge(b_done, min(g + 3, NG) if isinstance(i, int) else g + 3)
                            dve.tensor_scalar(below[:], xb[:, 0, :], final[:, bass.ds(i, 1)], None, ALU.max).then_inc(h_done, 1)
                        if there(i, u, 0):
                            dve.wait_ge(c_done, g + 1)
                            after(dve, o_done, g - 1)
                            dve.tensor_tensor(conv[:, u % 2], ps_c[u % 2][:], wscale[:].rearrange("p r c -> p (r c)"),
                                              ALU.mult).then_inc(m_done, 1)

                    run_groups(dve, step)

                @block.gpsimd
                def _(pool):
                    def step(i, u):
                        g = GPI * i + u
                        if there(i, u, 0):
                            pool.wait_ge(m_done, g + 1)
                            after(pool, s_out[u % 4], 16 * (2 * i + u // 4))
                            pool.tensor_tensor(o_s[:, u % 4].rearrange("p r c -> p (r c)"), conv[:, u % 2],
                                               x1[:, u].rearrange("p r c -> p (r c)"), ALU.add).then_inc(o_done, 1)

                    run_groups(pool, step)


_INS = ['x', 'L0_conv_w_qkv', 'L0_conv_w_v', 'L0_conv_w_proj', 'L1_conv_gamma', 'L1_conv_beta', 'L1_conv_W']


def kernel(**inputs):
    import numpy as _np
    import concourse.bacc as _bacc
    from concourse import mybir as _mybir
    from concourse.bass_utils import run_bass_kernel_spmd as _run

    nc = _bacc.Bacc("TRN2", target_bir_lowering=False, num_devices=1)
    arrays, args = {}, []
    for name in _INS:
        a = _np.ascontiguousarray(inputs[name])
        arrays[f"in_{name}"] = a
        args.append(nc.dram_tensor(f"in_{name}", a.shape, _mybir.dt.from_np(a.dtype), kind="ExternalInput").ap())
    out = nc.dram_tensor("out_0", inputs["x"].shape, F32, kind="ExternalOutput").ap()
    build_kernel(nc, *args, out)
    r = _run(nc, [arrays], core_ids=[0])
    return r.results[0]["out_0"]
```
